# Optimizing a Trainium2 kernel written in Bass

```python
import numpy as np
import jax
import jax.numpy as jnp

def _softmax(x, axis=-1):
    return jax.nn.softmax(x, axis=axis)

def _gelu(x):
    return jax.nn.gelu(x, approximate=True)

def _silu(x):
    return jax.nn.silu(x)

def _sigmoid(x):
    return jax.nn.sigmoid(x)

def _layernorm(x, axis=-1, eps=1e-05):
    m = jnp.mean(x, axis=axis, keepdims=True)
    v = jnp.var(x, axis=axis, keepdims=True)
    return (x - m) / jnp.sqrt(v + eps)

def _scatter_add(tgt, idx, src, axis=0):
    return tgt.at[idx].add(src)

def _segment_sum(src, seg, n):
    return jax.ops.segment_sum(src, seg, n)
kernel_name = 'mk_dlrm_tower_d1_rec_r8_890407'

def setup_inputs(seed: int=0):
    np.random.seed(seed)
    _w = jnp.asarray

    def _rec_inputs():
        import jax
        import jax.numpy as jnp
        _tk = jax.random.key(seed)
        dense_ctx = jax.random.normal(jax.random.fold_in(_tk, 190), (512, 16), jnp.float32)
        ids = jnp.stack([jax.random.randint(jax.random.fold_in(_tk, 200 + f), (512,), 0, v, jnp.int32) for f, v in enumerate([1250, 125000, 125000, 125000, 12500, 12500, 1250, 1250, 125000, 12500, 12500, 125000, 12500, 1000, 125000, 1000, 12500, 125000, 1000, 12500, 1000, 1000, 1000, 1000, 1250, 1000, 1250, 1000, 1000, 1000, 1250, 1250])], axis=1)
        tbl_0 = 0.05 * jax.random.normal(jax.random.fold_in(_tk, 500 + 0), (1250, 32), jnp.float32)
        tbl_1 = 0.05 * jax.random.normal(jax.random.fold_in(_tk, 500 + 1), (125000, 32), jnp.float32)
        tbl_2 = 0.05 * jax.random.normal(jax.random.fold_in(_tk, 500 + 2), (125000, 32), jnp.float32)
        tbl_3 = 0.05 * jax.random.normal(jax.random.fold_in(_tk, 500 + 3), (125000, 32), jnp.float32)
        tbl_4 = 0.05 * jax.random.normal(jax.random.fold_in(_tk, 500 + 4), (12500, 32), jnp.float32)
        tbl_5 = 0.05 * jax.random.normal(jax.random.fold_in(_tk, 500 + 5), (12500, 32), jnp.float32)
        tbl_6 = 0.05 * jax.random.normal(jax.random.fold_in(_tk, 500 + 6), (1250, 32), jnp.float32)
        tbl_7 = 0.05 * jax.random.normal(jax.random.fold_in(_tk, 500 + 7), (1250, 32), jnp.float32)
        tbl_8 = 0.05 * jax.random.normal(jax.random.fold_in(_tk, 500 + 8), (125000, 32), jnp.float32)
        tbl_9 = 0.05 * jax.random.normal(jax.random.fold_in(_tk, 500 + 9), (12500, 32), jnp.float32)
        tbl_10 = 0.05 * jax.random.normal(jax.random.fold_in(_tk, 500 + 10), (12500, 32), jnp.float32)
        tbl_11 = 0.05 * jax.random.normal(jax.random.fold_in(_tk, 500 + 11), (125000, 32), jnp.float32)
        tbl_12 = 0.05 * jax.random.normal(jax.random.fold_in(_tk, 500 + 12), (12500, 32), jnp.float32)
        tbl_13 = 0.05 * jax.random.normal(jax.random.fold_in(_tk, 500 + 13), (1000, 32), jnp.float32)
        tbl_14 = 0.05 * jax.random.normal(jax.random.fold_in(_tk, 500 + 14), (125000, 32), jnp.float32)
        tbl_15 = 0.05 * jax.random.normal(jax.random.fold_in(_tk, 500 + 15), (1000, 32), jnp.float32)
        tbl_16 = 0.05 * jax.random.normal(jax.random.fold_in(_tk, 500 + 16), (12500, 32), jnp.float32)
        tbl_17 = 0.05 * jax.random.normal(jax.random.fold_in(_tk, 500 + 17), (125000, 32), jnp.float32)
        tbl_18 = 0.05 * jax.random.normal(jax.random.fold_in(_tk, 500 + 18), (1000, 32), jnp.float32)
        tbl_19 = 0.05 * jax.random.normal(jax.random.fold_in(_tk, 500 + 19), (12500, 32), jnp.float32)
        tbl_20 = 0.05 * jax.random.normal(jax.random.fold_in(_tk, 500 + 20), (1000, 32), jnp.float32)
        tbl_21 = 0.05 * jax.random.normal(jax.random.fold_in(_tk, 500 + 21), (1000, 32), jnp.float32)
        tbl_22 = 0.05 * jax.random.normal(jax.random.fold_in(_tk, 500 + 22), (1000, 32), jnp.float32)
        tbl_23 = 0.05 * jax.random.normal(jax.random.fold_in(_tk, 500 + 23), (1000, 32), jnp.float32)
        tbl_24 = 0.05 * jax.random.normal(jax.random.fold_in(_tk, 500 + 24), (1250, 32), jnp.float32)
        tbl_25 = 0.05 * jax.random.normal(jax.random.fold_in(_tk, 500 + 25), (1000, 32), jnp.float32)
        tbl_26 = 0.05 * jax.random.normal(jax.random.fold_in(_tk, 500 + 26), (1250, 32), jnp.float32)
        tbl_27 = 0.05 * jax.random.normal(jax.random.fold_in(_tk, 500 + 27), (1000, 32), jnp.float32)
        tbl_28 = 0.05 * jax.random.normal(jax.random.fold_in(_tk, 500 + 28), (1000, 32), jnp.float32)
        tbl_29 = 0.05 * jax.random.normal(jax.random.fold_in(_tk, 500 + 29), (1000, 32), jnp.float32)
        tbl_30 = 0.05 * jax.random.normal(jax.random.fold_in(_tk, 500 + 30), (1250, 32), jnp.float32)
        tbl_31 = 0.05 * jax.random.normal(jax.random.fold_in(_tk, 500 + 31), (1250, 32), jnp.float32)
        _rk = jax.random.fold_in(_tk, 7)
        W_top1 = 0.0606339 * jax.random.normal(jax.random.fold_in(_tk, 801), (272, 512), jnp.float32)
        W_top2 = 0.0441942 * jax.random.normal(jax.random.fold_in(_tk, 802), (512, 256), jnp.float32)
        W_top3 = 0.0625 * jax.random.normal(jax.random.fold_in(_tk, 803), (256, 1), jnp.float32)
        b_top1 = jnp.zeros((512,), jnp.float32)
        b_top2 = jnp.zeros((256,), jnp.float32)
        return (dense_ctx, ids, tbl_0, tbl_1, tbl_2, tbl_3, tbl_4, tbl_5, tbl_6, tbl_7, tbl_8, tbl_9, tbl_10, tbl_11, tbl_12, tbl_13, tbl_14, tbl_15, tbl_16, tbl_17, tbl_18, tbl_19, tbl_20, tbl_21, tbl_22, tbl_23, tbl_24, tbl_25, tbl_26, tbl_27, tbl_28, tbl_29, tbl_30, tbl_31, W_top1, b_top1, W_top2, b_top2, W_top3)
    dense_ctx, ids, tbl_0, tbl_1, tbl_2, tbl_3, tbl_4, tbl_5, tbl_6, tbl_7, tbl_8, tbl_9, tbl_10, tbl_11, tbl_12, tbl_13, tbl_14, tbl_15, tbl_16, tbl_17, tbl_18, tbl_19, tbl_20, tbl_21, tbl_22, tbl_23, tbl_24, tbl_25, tbl_26, tbl_27, tbl_28, tbl_29, tbl_30, tbl_31, W_top1, b_top1, W_top2, b_top2, W_top3 = _rec_inputs()

    def _L0_rec_setup():
        import jax, jax.numpy as jnp
        import numpy as np
        B, F, D = (512, 32, 32)
        LAYER_SIZE = [128, 128]

        def _cin_forward(inputs, filters):
            x0 = inputs
            prev = inputs
            outs = []
            for W in filters:
                z = jnp.einsum('bhd,bmd->bhmd', x0, prev)
                b, h, m, d = z.shape
                z = z.reshape(b, h * m, d)
                cur = jnp.einsum('bpd,pn->bnd', z, W[0])
                cur = jax.nn.relu(cur)
                prev = cur
                outs.append(cur)
            result = jnp.concatenate(outs, axis=1)
            return jnp.sum(result, axis=-1)
        key = jax.random.key(seed)
        k1, k2, k3 = jax.random.split(key, 3)
        inputs = jax.random.normal(k1, (B, F, D), dtype=jnp.float32)
        field_nums = [F] + LAYER_SIZE
        filter_0 = jax.random.normal(k2, (1, field_nums[0] * field_nums[0], field_nums[1]), dtype=jnp.float32) * 0.05
        filter_1 = jax.random.normal(k3, (1, field_nums[0] * field_nums[1], field_nums[2]), dtype=jnp.float32) * 0.05
        return {'inputs': inputs, 'filter_0': filter_0, 'filter_1': filter_1}
    _L0_rec_all = _L0_rec_setup()
    _L0_rec_in = {k: v for k, v in _L0_rec_all.items() if k in ('filter_0', 'filter_1')}
    del _L0_rec_all
    return {'dense_ctx': dense_ctx, 'ids': ids, 'tbl_0': tbl_0, 'tbl_1': tbl_1, 'tbl_2': tbl_2, 'tbl_3': tbl_3, 'tbl_4': tbl_4, 'tbl_5': tbl_5, 'tbl_6': tbl_6, 'tbl_7': tbl_7, 'tbl_8': tbl_8, 'tbl_9': tbl_9, 'tbl_10': tbl_10, 'tbl_11': tbl_11, 'tbl_12': tbl_12, 'tbl_13': tbl_13, 'tbl_14': tbl_14, 'tbl_15': tbl_15, 'tbl_16': tbl_16, 'tbl_17': tbl_17, 'tbl_18': tbl_18, 'tbl_19': tbl_19, 'tbl_20': tbl_20, 'tbl_21': tbl_21, 'tbl_22': tbl_22, 'tbl_23': tbl_23, 'tbl_24': tbl_24, 'tbl_25': tbl_25, 'tbl_26': tbl_26, 'tbl_27': tbl_27, 'tbl_28': tbl_28, 'tbl_29': tbl_29, 'tbl_30': tbl_30, 'tbl_31': tbl_31, 'W_top1': W_top1, 'b_top1': b_top1, 'W_top2': W_top2, 'b_top2': b_top2, 'W_top3': W_top3, 'L0_rec_filter_0': _L0_rec_in['filter_0'], 'L0_rec_filter_1': _L0_rec_in['filter_1']}

def reference(dense_ctx, ids, tbl_0, tbl_1, tbl_2, tbl_3, tbl_4, tbl_5, tbl_6, tbl_7, tbl_8, tbl_9, tbl_10, tbl_11, tbl_12, tbl_13, tbl_14, tbl_15, tbl_16, tbl_17, tbl_18, tbl_19, tbl_20, tbl_21, tbl_22, tbl_23, tbl_24, tbl_25, tbl_26, tbl_27, tbl_28, tbl_29, tbl_30, tbl_31, W_top1, b_top1, W_top2, b_top2, W_top3, L0_rec_filter_0, L0_rec_filter_1):
    import jax
    import jax.numpy as jnp

    def _L0_rec_ref(inputs, filter_0, filter_1):
        import jax, jax.numpy as jnp
        import numpy as np
        B, F, D = (512, 32, 32)
        LAYER_SIZE = [128, 128]

        def _cin_forward(inputs, filters):
            x0 = inputs
            prev = inputs
            outs = []
            for W in filters:
                z = jnp.einsum('bhd,bmd->bhmd', x0, prev)
                b, h, m, d = z.shape
                z = z.reshape(b, h * m, d)
                cur = jnp.einsum('bpd,pn->bnd', z, W[0])
                cur = jax.nn.relu(cur)
                prev = cur
                outs.append(cur)
            result = jnp.concatenate(outs, axis=1)
            return jnp.sum(result, axis=-1)
        return _cin_forward(inputs, (filter_0, filter_1))
    e = jnp.stack([tbl_0[ids[:, 0]], tbl_1[ids[:, 1]], tbl_2[ids[:, 2]], tbl_3[ids[:, 3]], tbl_4[ids[:, 4]], tbl_5[ids[:, 5]], tbl_6[ids[:, 6]], tbl_7[ids[:, 7]], tbl_8[ids[:, 8]], tbl_9[ids[:, 9]], tbl_10[ids[:, 10]], tbl_11[ids[:, 11]], tbl_12[ids[:, 12]], tbl_13[ids[:, 13]], tbl_14[ids[:, 14]], tbl_15[ids[:, 15]], tbl_16[ids[:, 16]], tbl_17[ids[:, 17]], tbl_18[ids[:, 18]], tbl_19[ids[:, 19]], tbl_20[ids[:, 20]], tbl_21[ids[:, 21]], tbl_22[ids[:, 22]], tbl_23[ids[:, 23]], tbl_24[ids[:, 24]], tbl_25[ids[:, 25]], tbl_26[ids[:, 26]], tbl_27[ids[:, 27]], tbl_28[ids[:, 28]], tbl_29[ids[:, 29]], tbl_30[ids[:, 30]], tbl_31[ids[:, 31]]], axis=1)
    z = _L0_rec_ref(e, L0_rec_filter_0, L0_rec_filter_1)
    z = z.reshape(z.shape[0], -1)
    h = jnp.concatenate([z, dense_ctx], axis=1)
    h = jnp.maximum(h @ W_top1 + b_top1, 0.0)
    h = jnp.maximum(h @ W_top2 + b_top2, 0.0)
    y = h @ W_top3
    return y

_drawn_inputs = setup_inputs


def setup_inputs(seed=0):
    import zlib

    import numpy as np

    out = dict(_drawn_inputs(seed))
    spreads = {'b_top1': (0.0, 0.432), 'b_top2': (0.0, 0.423)}
    factors = {'tbl_0': 5.844,
     'tbl_1': 6.294,
     'tbl_2': 5.84,
     'tbl_3': 6.175,
     'tbl_4': 5.98,
     'tbl_5': 5.976,
     'tbl_6': 6.192,
     'tbl_7': 6.382,
     'tbl_8': 5.933,
     'tbl_9': 6.174,
     'tbl_10': 5.99,
     'tbl_11': 6.07,
     'tbl_12': 6.333,
     'tbl_13': 6.006,
     'tbl_14': 6.258,
     'tbl_15': 5.945,
     'tbl_16': 5.934,
     'tbl_17': 6.024,
     'tbl_18': 5.974,
     'tbl_19': 5.743,
     'tbl_20': 5.589,
     'tbl_21': 6.279,
     'tbl_22': 6.007,
     'tbl_23': 6.174,
     'tbl_24': 6.567,
     'tbl_25': 6.182,
     'tbl_26': 5.928,
     'tbl_27': 5.877,
     'tbl_28': 6.042,
     'tbl_29': 6.025,
     'tbl_30': 6.646,
     'tbl_31': 5.858,
     'L0_rec_filter_1': 8.0}
    for name, (base, spread) in spreads.items():
        noise = np.random.default_rng([zlib.crc32(name.encode()), seed]).standard_normal(out[name].shape)
        drawn = base * np.exp(spread * noise) if base else spread * noise
        out[name] = jnp.asarray(drawn.astype(out[name].dtype))
    for name, factor in factors.items():
        out[name] = (out[name] * factor).astype(out[name].dtype)
    return out
```

```python
from contextlib import ExitStack

import numpy as np

import concourse.bass as bass
from concourse import mybir

F32 = mybir.dt.float32
F32R = mybir.dt.float32r
I32 = mybir.dt.int32
U32 = mybir.dt.uint32
ALU = mybir.AluOpType
ACT = mybir.ActivationFunctionType
AX = mybir.AxisListType

B, F, D, N, DENSE = 512, 32, 32, 128, 16
TOP1, TOP2 = 512, 256
P = 128
BT = P // D
TILES = B // BT
TG = 4
GROUPS = TILES // TG
COLS = TG * P
KP = 5
SH = P // F
BANK = 512
HB = BANK // N
NK = F // HB
RING = 6
SLOTS = 3
ACT_FIELDS = (4, 0, 4, 0, 4, 0, 4, 0)
ADD = 12
ADD_AFTER = (2 * ADD - 1) // HB


def after(counts, bank):
    return sum(1 for c in counts[:bank + 1] if c)


DVE_FIELDS = tuple(HB - a for a in ACT_FIELDS)


class Group:

    def __init__(self, i, r):
        self.i, self.r = (i if 0 <= r < SLOTS else i + r // SLOTS), r % SLOTS

    def plus(self, n):
        return Group(self.i, self.r + n)

    def times(self, k, add=0):
        return self.i * (SLOTS * k) + (self.r * k + add)

    def uses(self, k):
        return self.i * k + k


def wait(engine, semaphore, value):
    if not isinstance(value, int) or value > 0:
        engine.wait_ge(semaphore, value)


def over_groups(engine, body):
    body(Group(0, 0), 0)
    body(Group(0, 1), 1)
    loops = (GROUPS - 2) // SLOTS - 1
    with engine.Fori(0, loops) as i:
        for r in range(2, 2 + SLOTS):
            body(Group(i, r), None)
    for g in range(2 + SLOTS * loops, GROUPS):
        body(Group(g // SLOTS, g % SLOTS), g)


def tower(nc, ids, row_base, row_last, table, dense_t, w0a, w0b, w1, wt1, bt1, wt2, bt2, wt3, y):
    ctx = ExitStack()
    with ctx:
        def sb(name, shape, dt=F32):
            return ctx.enter_context(nc.sbuf_tensor(name, shape, dt))

        def sem(name):
            return ctx.enter_context(nc.semaphore(name))

        et = nc.dram_tensor("et_scratch", [2 * F, B * D], F32, kind="Internal").ap()

        ids_sb = sb("ids_sb", [P, TILES], I32)
        idf = sb("idf", [P, TILES])
        neg = sb("neg", [P, TILES])
        base_sb = sb("base_sb", [P, 1])
        last_sb = sb("last_sb", [P, 2])
        rows = sb("rows", [P, TILES], U32)
        rows_now = sb("rows_now", [P, SLOTS, TG], U32)
        gat = sb("gat", [P, SLOTS, TG * D])
        es = sb("es", [P, SLOTS, TG, F])
        first = sb("first", [P, SLOTS, COLS])
        second = sb("second", [P, SLOTS, KP, COLS])
        z = sb("z", [P, KP, COLS])
        z_hi = sb("z_hi", [P, KP, COLS], F32R)
        z_lo = sb("z_lo", [P, KP, COLS], F32R)
        c = sb("c", [P, COLS])
        c_hi = sb("c_hi", [P, SLOTS, COLS], F32R)
        c_lo = sb("c_lo", [P, SLOTS, COLS], F32R)
        w0_hi = sb("w0_hi", [P, KP, N], F32R)
        w0_lo = sb("w0_lo", [P, KP, N], F32R)
        w1_hi = sb("w1_hi", [P, F, N], F32R)
        w1_lo = sb("w1_lo", [P, F, N], F32R)
        prod = sb("prod", [P, 2, F, N])
        csum = sb("csum", [P, N])
        c1 = sb("c1", [P, 2, N])
        ones_b = sb("ones_b", [P, BT])
        h0 = sb("h0", [P, B])
        h1 = sb("h1", [P, B])
        hd = sb("hd", [DENSE, B])
        wt1_sb = sb("wt1_sb", [P, 2, TOP1])
        wt1_d = sb("wt1_d", [DENSE, TOP1])
        bt1_sb = sb("bt1_sb", [P, TOP1 // P])
        wt2_sb = sb("wt2_sb", [P, TOP1 // P, TOP2])
        bt2_sb = sb("bt2_sb", [P, TOP2 // P])
        wt3_sb = sb("wt3_sb", [P, TOP2 // P])
        y_sb = sb("y_sb", [1, B])
        w1_raw = prod[:, 0, :, :]
        w0a_sb = prod[:, 1, 0:KP, :]
        w0b_sb = prod[:, 1, KP:2 * KP, :]
        w0_sum = prod[:, 1, 2 * KP:3 * KP, :]
        a1 = z[:, 0:4, :]
        a2 = second[:, 0, 0:2, :]

        ps_y = ctx.enter_context(nc.psum_tensor("ps_y", [P, RING, BANK], F32))
        ps_c = ctx.enter_context(nc.psum_tensor("ps_c", [P, COLS], F32))
        ps_h1 = ctx.enter_context(nc.psum_tensor("ps_h1", [P, B], F32))

        ids_in = sem("ids_in")
        w0_in = sem("w0_in")
        w1_in = sem("w1_in")
        top_in = sem("top_in")
        rows_step = sem("rows_step")
        w_ready = sem("w_ready")
        w1_hi_ready = sem("w1_hi_ready")
        w0_step = sem("w0_step")
        ones_zeroed = sem("ones_zeroed")
        rows_staged = sem("rows_staged")
        pool_passed = sem("pool_passed")
        sp_passed = sem("sp_passed")
        gathered = [sem(f"gathered{s}") for s in range(SLOTS)]
        et_written = sem("et_written")
        pairs_in = [sem(f"pairs_in{s}") for s in range(SLOTS)]
        es_ready = sem("es_ready")
        z_ready = sem("z_ready")
        z_hi_ready = sem("z_hi_ready")
        z_lo_ready = sem("z_lo_ready")
        l0_done = sem("l0_done")
        c_ready = sem("c_ready")
        c_hi_ready = sem("c_hi_ready")
        c_lo_ready = sem("c_lo_ready")
        h0_done = sem("h0_done")
        y_ready = sem("y_ready")
        act_scaled = sem("act_scaled")
        dve_scaled = sem("dve_scaled")
        added = sem("added")
        reduced = sem("reduced")
        c1_ready = sem("c1_ready")
        h1_done = sem("h1_done")
        h1_copied = sem("h1_copied")
        mm_top = sem("mm_top")
        act_top = sem("act_top")
        y_out = sem("y_out")

        block = ctx.enter_context(nc.Block())

        def act_count(g, u, k):
            u, k = u + k // NK, k % NK
            return g.times(TG * after(ACT_FIELDS, NK), u * after(ACT_FIELDS, NK) + after(ACT_FIELDS, k))

        def dve_count(g, u, k):
            u, k = u + k // NK, k % NK
            return g.times(TG * after(DVE_FIELDS, NK), u * after(DVE_FIELDS, NK) + after(DVE_FIELDS, k))

        def bank_of(g, u, k):
            return (NK * (TG * g.r + u) + k) % RING

        @block.sync
        def _(sp):
            sp.dma_start(ids_sb[:, :], ids).then_inc(ids_in, 16)
            sp.dma_start(base_sb[:, :], row_base).then_inc(ids_in, 16)
            sp.dma_start(last_sb[:, :], row_last).then_inc(ids_in, 16)
            sp.dma_start(w0a_sb, w0a).then_inc(w0_in, 16)
            sp.dma_start(w0b_sb, w0b).then_inc(w0_in, 16)
            sp.dma_start(w1_raw, w1.rearrange("(h m) n -> m h n", m=N)).then_inc(w1_in, 16)

            def pairs(g):
                cols = g.times(COLS)
                sp.wait_ge(gathered[g.r], g.uses(16 * TG))
                sp.sem_inc(sp_passed, 1)
                for b in range(BT):
                    here = et.rearrange("(two f) c -> f two c", two=2)[:, :, bass.ds(cols + b * TG * D, TG * D)]
                    src = gat[b * F:(b + 1) * F, g.r, :].unsqueeze(1).to_broadcast([F, 2, TG * D])
                    sp.dma_start(here, src).then_inc(et_written, 16)
                sp.wait_ge(et_written, g.times(16 * BT, 16 * BT))
                sp.sem_inc(sp_passed, 1)
                wait(sp, z_ready, g.times(KP, -KP * (SLOTS - 1)))
                sp.sem_inc(sp_passed, 1)
                row = B * D
                lead = et[0:1, bass.ds(cols, COLS)]

                def shifted(rows_on, step):
                    return bass.AP(tensor=lead.tensor, offset=lead.offset + rows_on * row,
                                   ap=[[row, F], [step, SH], [1, COLS]])

                sp.dma_start(first[:, g.r, :], shifted(0, 0)).then_inc(pairs_in[g.r], 16)
                for k in range(KP):
                    sp.dma_start(second[:, g.r, k, :], shifted(SH * k, row)).then_inc(pairs_in[g.r], 16)

            for g in range(SLOTS):
                pairs(Group(0, g))
            sp.dma_start(wt1_sb[:, :, :], wt1[0:2 * P, :].rearrange("(k p) n -> p k n", p=P)).then_inc(top_in, 16)
            sp.dma_start(wt1_d[:, :], wt1[2 * P:2 * P + DENSE, :]).then_inc(top_in, 16)
            sp.dma_start(wt2_sb[:, :, :], wt2.rearrange("(k p) n -> p k n", p=P)).then_inc(top_in, 16)
            sp.dma_start(wt3_sb[:, :], wt3).then_inc(top_in, 16)
            sp.dma_start(bt1_sb[:, :], bt1).then_inc(top_in, 16)
            sp.dma_start(bt2_sb[:, :], bt2).then_inc(top_in, 16)
            sp.dma_start(hd[:, :], dense_t).then_inc(top_in, 16)

            def body(g, number):
                if number is None or number + SLOTS < GROUPS:
                    pairs(g.plus(SLOTS))

            over_groups(sp, body)
            sp.wait_ge(act_top, 7)
            sp.dma_start(y, y_sb[:, :]).then_inc(y_out, 16)
            sp.wait_ge(y_out, 16)

        @block.gpsimd
        def _(pool):
            def gather(g):
                if not isinstance(g.i, int) or g.i > 0:
                    pool.wait_ge(es_ready, g.times(1, 1 - SLOTS))
                    pool.wait_ge(et_written, g.times(16 * BT, 16 * BT * (1 - SLOTS)))
                nc.gpsimd.tensor_copy(rows_now[:, g.r, :], rows[:, bass.ds(g.times(TG), TG)]).then_inc(rows_staged, 1)
                pool.wait_ge(rows_staged, g.times(1, 1))
                pool.sem_inc(pool_passed, 1)
                for u in range(TG):
                    pool.indirect_dma_start(
                        out=gat[:, g.r, u * D:(u + 1) * D], out_offset=None, in_=table,
                        in_offset=bass.IndirectOffsetOnAxis(ap=rows_now[:, g.r, u:u + 1], axis=0),
                    ).then_inc(gathered[g.r], 16)

            def split_z(g, k):
                pool.wait_ge(z_hi_ready, g.times(KP, k + 1))
                wait(pool, l0_done, g.times(1))
                nc.gpsimd.tensor_tensor(z_lo[:, k, :], z[:, k, :], z_hi[:, k, :].bitcast(F32),
                                        ALU.subtract).then_inc(z_lo_ready, 1)

            def add(g, u):
                pool.wait_ge(act_scaled, act_count(g, u, ADD_AFTER))
                pool.wait_ge(dve_scaled, dve_count(g, u, ADD_AFTER))
                low, high = prod[:, u % 2, 0:ADD, :], prod[:, u % 2, ADD:2 * ADD, :]
                nc.gpsimd.tensor_tensor(high, high, low, ALU.add).then_inc(added, 1)

            pool.wait_ge(rows_step, 5)
            for g in range(SLOTS):
                gather(Group(0, g))
            for k in range(KP):
                split_z(Group(0, 0), k)

            def body(g, number):
                more = number is None or number + 1 < GROUPS
                for u in range(TG):
                    if more:
                        for k in ((0, 1), (2, 3), (4,), ())[u]:
                            split_z(g.plus(1), k)
                    if u == 2 and (number is None or number + SLOTS < GROUPS):
                        gather(g.plus(SLOTS))
                    add(g, u)

            over_groups(pool, body)

        @block.scalar
        def _(act):
            def split_z(g, k):
                act.wait_ge(z_ready, g.times(KP, k + 1))
                wait(act, l0_done, g.times(1))
                nc.scalar.activation(z_hi[:, k, :], z[:, k, :], ACT.Copy).then_inc(z_hi_ready, 1)

            def rectify(g):
                act.wait_ge(l0_done, g.times(1, 1))
                wait(act, h0_done, g.times(1))
                nc.scalar.activation(c[:, :], ps_c[:, :], ACT.Relu).then_inc(c_ready, 1)
                nc.scalar.activation(
                    c_hi[:, g.r, :].rearrange("p (u b d) -> p b u d", u=TG, b=BT),
                    ps_c[:, :].rearrange("p (b u d) -> p b u d", u=TG, b=BT), ACT.Relu,
                ).then_inc(c_hi_ready, 1)

            def scale(g, u, k, number):
                if not ACT_FIELDS[k]:
                    return
                if after(ACT_FIELDS, k) == 1:
                    if u == 0:
                        act.wait_ge(es_ready, g.times(1, 1))
                    wait(act, reduced, g.times(TG, u - 1))
                act.wait_ge(y_ready, g.times(TG * NK, u * NK + k + 1))
                for j in range(ACT_FIELDS[k]):
                    h = HB * k + j
                    last = nc.scalar.activation(prod[:, u % 2, h, :],
                                                ps_y[:, bank_of(g, u, k), j * N:(j + 1) * N], ACT.Copy,
                                                scale=es[:, g.r, u, h:h + 1])
                last.then_inc(act_scaled, 1)

            act.wait_ge(w1_in, 16)
            for k in range(NK):
                nc.scalar.activation(w1_hi[:, k * HB:(k + 1) * HB, :], w1_raw[:, k * HB:(k + 1) * HB, :],
                                     ACT.Copy).then_inc(w1_hi_ready, 1)
            for k in range(KP):
                split_z(Group(0, 0), k)
            rectify(Group(0, 0))
            act.wait_ge(w_ready, 2)

            def body(g, number):
                more = number is None or number + 1 < GROUPS
                for u in range(TG):
                    for k in range(NK):
                        scale(g, u, k, number)
                        if more and (u, k) in Z_HI_AT:
                            split_z(g.plus(1), Z_HI_AT.index((u, k)))
                        if more and (u, k) == (3, 2):
                            rectify(g.plus(1))

            Z_HI_AT = ((0, 1), (0, 4), (0, 7), (1, 2), (1, 5))
            over_groups(act, body)

            act.wait_ge(h1_done, TILES)
            nc.scalar.activation(h1[:, :], ps_h1[:, :], ACT.Copy).then_inc(h1_copied, 1)
            act.wait_ge(top_in, 7 * 16)
            for j in range(TOP1 // P):
                act.wait_ge(mm_top, j + 1)
                nc.scalar.activation(a1[:, j, :], ps_y[:, j, :], ACT.Relu, bias=bt1_sb[:, j:j + 1]).then_inc(act_top, 1)
            for j in range(TOP2 // P):
                act.wait_ge(mm_top, 5 + j)
                nc.scalar.activation(a2[:, j, :], ps_y[:, 4 + j, :], ACT.Relu, bias=bt2_sb[:, j:j + 1]).then_inc(act_top, 1)
            act.wait_ge(mm_top, 7)
            nc.scalar.activation(y_sb[:, :], ps_c[0:1, :], ACT.Copy).then_inc(act_top, 1)

        @block.vector
        def _(dve):
            dve.wait_ge(ids_in, 48)
            nc.vector.tensor_copy(idf[:, :], ids_sb[:, :]).then_inc(rows_step, 1)
            dve.wait_ge(rows_step, 1)
            nc.vector.tensor_scalar(neg[:, :], idf[:, :], 0.0, last_sb[:, 1:2], ALU.is_lt, ALU.mult).then_inc(rows_step, 1)
            dve.wait_ge(rows_step, 2)
            nc.vector.tensor_tensor(idf[:, :], idf[:, :], neg[:, :], ALU.add).then_inc(rows_step, 1)
            dve.wait_ge(rows_step, 3)
            nc.vector.tensor_scalar(neg[:, :], idf[:, :], 0.0, last_sb[:, 0:1], ALU.max, ALU.min).then_inc(rows_step, 1)
            dve.wait_ge(rows_step, 4)
            nc.vector.tensor_scalar(rows[:, :], neg[:, :], base_sb[:, 0:1], None, ALU.add).then_inc(rows_step, 1)

            nc.vector.memset(ones_b[:, :], 0.0).then_inc(ones_zeroed, 1)
            dve.wait_ge(ones_zeroed, 1)
            for b in range(BT):
                nc.vector.memset(ones_b[b * D:(b + 1) * D, b:b + 1], 1.0).then_inc(ones_zeroed, 1)

            dve.wait_ge(w0_in, 32)
            nc.vector.tensor_tensor(w0_sum, w0a_sb, w0b_sb, ALU.add).then_inc(w0_step, 1)
            dve.wait_ge(w0_step, 1)
            nc.vector.tensor_copy(w0_hi[:, :, :], w0_sum).then_inc(w0_step, 1)
            dve.wait_ge(w0_step, 2)
            nc.vector.tensor_tensor(w0_lo[:, :, :], w0_sum, w0_hi[:, :, :].bitcast(F32), ALU.subtract).then_inc(w_ready, 1)

            def turn(g):
                dve.wait_ge(gathered[g.r], g.uses(16 * TG))
                nc.vector.transpose(es[:, g.r, :, :].rearrange("p u f -> p (u f)"), gat[:, g.r, :]).then_inc(es_ready, 1)

            def multiply(g, k):
                if k == 0:
                    dve.wait_ge(pairs_in[g.r], g.uses(16 * (KP + 1)))
                wait(dve, z_hi_ready, g.times(KP, k + 1 - KP))
                wait(dve, z_lo_ready, g.times(KP, k + 1 - KP))
                nc.vector.tensor_tensor(z[:, k, :], first[:, g.r, :], second[:, g.r, k, :], ALU.mult).then_inc(z_ready, 1)

            def split_c(g):
                dve.wait_ge(c_hi_ready, g.times(1, 1))
                nc.vector.tensor_tensor(
                    c_lo[:, g.r, :].rearrange("p (u b d) -> p b u d", u=TG, b=BT),
                    c[:, :].rearrange("p (b u d) -> p b u d", u=TG, b=BT),
                    c_hi[:, g.r, :].bitcast(F32).rearrange("p (u b d) -> p b u d", u=TG, b=BT),
                    ALU.subtract).then_inc(c_lo_ready, 1)

            def sum_h0(g):
                nc.vector.tensor_reduce(
                    h0[:, bass.ds(g.times(TG * BT), TG * BT)].rearrange("p (u b) -> p b u", u=TG),
                    c[:, :].rearrange("p (b u d) -> p b u d", u=TG, b=BT), AX.X, ALU.add).then_inc(h0_done, 1)

            def scale(g, u, k):
                n = DVE_FIELDS[k]
                if not n:
                    return
                if after(DVE_FIELDS, k) == 1:
                    if u == 0:
                        dve.wait_ge(es_ready, g.times(1, 1))
                    wait(dve, reduced, g.times(TG, u - 1))
                dve.wait_ge(y_ready, g.times(TG * NK, u * NK + k + 1))
                h = HB * k + HB - n
                nc.vector.tensor_tensor(
                    prod[:, u % 2, h:h + n, :],
                    ps_y[:, bank_of(g, u, k), (HB - n) * N:].rearrange("p (h n) -> p h n", n=N),
                    es[:, g.r, u, h:h + n].unsqueeze(2).to_broadcast([P, n, N]), ALU.mult).then_inc(dve_scaled, 1)

            def reduce(g, u):
                dve.wait_ge(added, g.times(TG, u + 1))
                dve.wait_ge(act_scaled, act_count(g, u, NK - 1))
                dve.wait_ge(dve_scaled, dve_count(g, u, NK - 1))
                nc.vector.tensor_reduce(csum[:, :], prod[:, u % 2, ADD:F, :].rearrange("p h n -> p n h"),
                                        AX.X, ALU.add).then_inc(reduced, 1)
                dve.wait_ge(reduced, g.times(TG, u + 1))
                wait(dve, h1_done, g.times(TG, u - 1))
                nc.vector.tensor_scalar(c1[:, u % 2, :], csum[:, :], 0.0, None, ALU.max).then_inc(c1_ready, 1)

            turn(Group(0, 0))
            for k in range(KP):
                multiply(Group(0, 0), k)
            for k in range(NK):
                dve.wait_ge(w1_hi_ready, k + 1)
                part = slice(k * HB, (k + 1) * HB)
                last = nc.vector.tensor_tensor(w1_lo[:, part, :], w1_raw[:, part, :],
                                               w1_hi[:, part, :].bitcast(F32), ALU.subtract)
            last.then_inc(w_ready, 1)
            split_c(Group(0, 0))
            sum_h0(Group(0, 0))
            dve.wait_ge(w_ready, 2)

            Z_AT = ((0, 1), (0, 3), (0, 5), (0, 7), (1, 1))

            def body(g, number):
                more = number is None or number + 1 < GROUPS
                for u in range(TG):
                    for k in range(NK):
                        scale(g, u, k)
                        if k == 3 and not (number == 0 and u == 0):
                            reduce(*((g.plus(-1), TG - 1) if u == 0 else (g, u - 1)))
                        if more and (u, k) in Z_AT:
                            multiply(g.plus(1), Z_AT.index((u, k)))
                        if more and (u, k) == (1, 5):
                            turn(g.plus(1))
                        if more and (u, k) == (3, 5):
                            split_c(g.plus(1))
                            sum_h0(g.plus(1))

            over_groups(dve, body)
            reduce(Group((GROUPS - 1) // SLOTS, (GROUPS - 1) % SLOTS), TG - 1)

        @block.tensor
        def _(pe):
            def layer0(g, k):
                if k == 0:
                    wait(pe, c_hi_ready, g.times(1))
                pe.wait_ge(z_hi_ready, g.times(KP, k + 1))
                pe.wait_ge(z_lo_ready, g.times(KP, k + 1))
                nc.tensor.matmul(ps_c[:, :], w0_hi[:, k, :], z_hi[:, k, :], start=(k == 0), stop=False)
                nc.tensor.matmul(ps_c[:, :], w0_lo[:, k, :], z_hi[:, k, :], start=False, stop=False)
                last = nc.tensor.matmul(ps_c[:, :], w0_hi[:, k, :], z_lo[:, k, :], start=False, stop=(k == KP - 1))
                if k == KP - 1:
                    last.then_inc(l0_done, 1)

            def layer1(g, u, k, number):
                if number is None or number > 0 or NK * u + k >= RING:
                    wait(pe, act_scaled, act_count(g, u, k - RING))
                    wait(pe, dve_scaled, dve_count(g, u, k - RING))
                out = ps_y[:, bank_of(g, u, k), :]
                hi, lo = (x[:, g.r, u * P:(u + 1) * P] for x in (c_hi, c_lo))
                w_hi, w_lo = (x[:, k * HB:(k + 1) * HB, :].rearrange("p h n -> p (h n)") for x in (w1_hi, w1_lo))
                nc.tensor.matmul(out, hi, w_hi, start=True, stop=False)
                nc.tensor.matmul(out, hi, w_lo, start=False, stop=False)
                nc.tensor.matmul(out, lo, w_hi, start=False, stop=True).then_inc(y_ready, 1)

            def sum_h1(g, u):
                pe.wait_ge(c1_ready, g.times(TG, u + 1))
                nc.tensor.matmul(ps_h1[:, bass.ds(g.times(TG * BT, u * BT), BT)], c1[:, u % 2, :], ones_b[:, :],
                                 start=True, stop=True).then_inc(h1_done, 1)

            pe.wait_ge(ones_zeroed, 1 + BT)
            pe.wait_ge(w_ready, 1)
            for k in range(KP):
                layer0(Group(0, 0), k)
            pe.wait_ge(w_ready, 2)

            Z_USED_AT = ((1, 3), (1, 6), (2, 1), (2, 4), (2, 7))

            def body(g, number):
                more = number is None or number + 1 < GROUPS
                pe.wait_ge(c_hi_ready, g.times(1, 1))
                pe.wait_ge(c_lo_ready, g.times(1, 1))
                for u in range(TG):
                    for k in range(NK):
                        layer1(g, u, k, number)
                        if more and (u, k) in Z_USED_AT:
                            layer0(g.plus(1), Z_USED_AT.index((u, k)))
                        if k == NK - 1 and not (number == 0 and u == 0):
                            sum_h1(*((g.plus(-1), TG - 1) if u == 0 else (g, u - 1)))

            over_groups(pe, body)
            sum_h1(Group((GROUPS - 1) // SLOTS, (GROUPS - 1) % SLOTS), TG - 1)

            pe.wait_ge(top_in, 7 * 16)
            pe.wait_ge(h0_done, GROUPS)
            pe.wait_ge(h1_copied, 1)
            for j in range(TOP1 // P):
                cols = slice(j * P, (j + 1) * P)
                nc.tensor.matmul(ps_y[:, j, :], wt1_sb[:, 0, cols], h0[:, :], start=True, stop=False)
                nc.tensor.matmul(ps_y[:, j, :], wt1_d[:, cols], hd[:, :], start=False, stop=False)
                nc.tensor.matmul(ps_y[:, j, :], wt1_sb[:, 1, cols], h1[:, :], start=False, stop=True).then_inc(mm_top, 1)
            for k in range(TOP1 // P):
                pe.wait_ge(act_top, k + 1)
                for j in range(TOP2 // P):
                    last = nc.tensor.matmul(ps_y[:, 4 + j, :], wt2_sb[:, k, j * P:(j + 1) * P], a1[:, k, :],
                                            start=(k == 0), stop=(k == TOP1 // P - 1))
                    if k == TOP1 // P - 1:
                        last.then_inc(mm_top, 1)
            for k in range(TOP2 // P):
                pe.wait_ge(act_top, TOP1 // P + k + 1)
                last = nc.tensor.matmul(ps_c[0:1, :], wt3_sb[:, k:k + 1], a2[:, k, :],
                                        start=(k == 0), stop=(k == TOP2 // P - 1))
            last.then_inc(mm_top, 1)


def pair_rows():
    a = np.full((F, SH, KP), F * F)
    b = np.full((F, SH, KP), F * F)
    for k in range(KP):
        for s in range(SH):
            dist = SH * k + s
            for h in range(F):
                m = (h + dist) % F
                if dist < F // 2 or (dist == F // 2 and h < F // 2):
                    a[h, s, k] = F * h + m
                    if dist:
                        b[h, s, k] = F * m + h
    return a.reshape(P, KP), b.reshape(P, KP)


def kernel(**inputs):
    import concourse.bacc as bacc
    from concourse.bass_utils import run_bass_kernel_spmd

    x = {name: np.asarray(a) for name, a in inputs.items()}
    tables = [x[f"tbl_{f}"] for f in range(F)]
    counts = np.array([t.shape[0] for t in tables])
    bases = np.cumsum(counts) - counts
    rows_a, rows_b = pair_rows()
    w0 = np.concatenate([x["L0_rec_filter_0"][0], np.zeros((1, N), np.float32)])
    arrays = {
        "ids": np.ascontiguousarray(x["ids"].reshape(TILES, BT, F).transpose(1, 2, 0).reshape(P, TILES)),
        "row_base": np.tile(bases.astype(np.float32), BT).reshape(P, 1),
        "row_last": np.tile(np.stack([counts - 1, counts], 1).astype(np.float32), (BT, 1)),
        "table": np.concatenate(tables),
        "dense_t": np.ascontiguousarray(x["dense_ctx"].T),
        "w0a": w0[rows_a],
        "w0b": w0[rows_b],
        "w1": np.ascontiguousarray(x["L0_rec_filter_1"][0]),
        "wt1": x["W_top1"],
        "bt1": np.ascontiguousarray(x["b_top1"].reshape(TOP1 // P, P).T),
        "wt2": x["W_top2"],
        "bt2": np.ascontiguousarray(x["b_top2"].reshape(TOP2 // P, P).T),
        "wt3": np.ascontiguousarray(x["W_top3"].reshape(TOP2 // P, P).T),
    }
    nc = bacc.Bacc("TRN2", target_bir_lowering=False, num_devices=1)
    args = [nc.dram_tensor(n, a.shape, mybir.dt.from_np(a.dtype), kind="ExternalInput").ap() for n, a in arrays.items()]
    y = nc.dram_tensor("y", (1, B), F32, kind="ExternalOutput").ap()
    tower(nc, *args, y)
    r = run_bass_kernel_spmd(nc, [arrays], core_ids=[0])
    return r.results[0]["y"].reshape(B, 1)
```

```python
from contextlib import ExitStack

import numpy as np

import concourse.bass as bass
from concourse import mybir

F32 = mybir.dt.float32
F32R = mybir.dt.float32r
I32 = mybir.dt.int32
U32 = mybir.dt.uint32
ALU = mybir.AluOpType
ACT = mybir.ActivationFunctionType
AX = mybir.AxisListType

B, F, D, N, DENSE = 512, 32, 32, 128, 16
TOP1, TOP2 = 512, 256
P = 128
BT = P // D
TILES = B // BT
TG = 4
GROUPS = TILES // TG
COLS = TG * P
KP = 5
SH = P // F
BANK = 512
HB = BANK // N
NK = F // HB
RING = 6
SLOTS = 3
BUFS = 3
KS = KP - 1
ACT_BANKS = ((0, 2, 3, 5, 7), (0, 2, 3, 5, 7), (0, 2, 3, 5, 7), (0, 2, 4, 6))
DVE_BANKS = tuple(tuple(k for k in range(NK) if k not in a) for a in ACT_BANKS)
ADD = 12
ADD_AFTER = (2 * ADD - 1) // HB
HALVES = 2


def signals(banks, g, u, k):
    if k < 0:
        g, u, k = (g, u - 1, k + NK) if u else (g.plus(-1), TG - 1, k + NK)
    return g.times(sum(map(len, banks)), sum(map(len, banks[:u])) + sum(x <= k for x in banks[u]))


class Group:

    def __init__(self, i, r):
        self.i, self.r = (i if 0 <= r < SLOTS else i + r // SLOTS), r % SLOTS

    def plus(self, n):
        return Group(self.i, self.r + n)

    def times(self, k, add=0):
        return self.i * (SLOTS * k) + (self.r * k + add)

    def uses(self, k):
        return self.i * k + k


def wait(engine, semaphore, value):
    if not isinstance(value, int) or value > 0:
        engine.wait_ge(semaphore, value)


def over_groups(engine, body):
    body(Group(0, 0), 0)
    body(Group(0, 1), 1)
    loops = (GROUPS - 2) // SLOTS - 1
    with engine.Fori(0, loops) as i:
        for r in range(2, 2 + SLOTS):
            body(Group(i, r), None)
    for g in range(2 + SLOTS * loops, GROUPS):
        body(Group(g // SLOTS, g % SLOTS), g)


LAST = Group((GROUPS - 1) // SLOTS, (GROUPS - 1) % SLOTS)


def tower(nc, ids, row_base, row_last, table, dense_t, w0a, w0b, w1, wt1, bt1, wt2, bt2, wt3, y):
    ctx = ExitStack()
    with ctx:
        def sb(name, shape, dt=F32):
            return ctx.enter_context(nc.sbuf_tensor(name, shape, dt))

        def sem(name):
            return ctx.enter_context(nc.semaphore(name))

        et = nc.dram_tensor("et_scratch", [2 * F, B * D], F32, kind="Internal").ap()

        ids_sb = sb("ids_sb", [P, TILES], I32)
        idf = sb("idf", [P, TILES])
        neg = sb("neg", [P, TILES])
        base_sb = sb("base_sb", [P, 1])
        last_sb = sb("last_sb", [P, 2])
        rows = sb("rows", [P, TILES], U32)
        rows_now = sb("rows_now", [P, SLOTS, TG], U32)
        gat = sb("gat", [P, SLOTS, TG * D])
        es = sb("es", [P, SLOTS, TG, F])
        first = sb("first", [P, COLS])
        second = sb("second", [P, KP, COLS])
        z = sb("z", [P, KP, COLS])
        z_hi = sb("z_hi", [P, KS, COLS], F32R)
        z_lo = sb("z_lo", [P, KS, COLS], F32R)
        c = sb("c", [P, COLS])
        c_hi = sb("c_hi", [P, SLOTS, COLS], F32R)
        c_lo = sb("c_lo", [P, SLOTS, COLS], F32R)
        w0_sum = sb("w0_sum", [P, KP, N])
        w0_hi = sb("w0_hi", [P, KS, N], F32R)
        w0_lo = sb("w0_lo", [P, KS, N], F32R)
        w1_hi = sb("w1_hi", [P, F, N], F32R)
        w1_lo = sb("w1_lo", [P, F, N], F32R)
        prod = sb("prod", [P, BUFS, F, N])
        csum = sb("csum", [P, N])
        c1 = sb("c1", [P, 2, N])
        ones_b = sb("ones_b", [P, BT])
        h0 = sb("h0", [P, B])
        h1 = sb("h1", [P, B])
        hd = sb("hd", [DENSE, B])
        wt1_sb = sb("wt1_sb", [P, 2, TOP1])
        wt1_d = sb("wt1_d", [DENSE, TOP1])
        bt1_sb = sb("bt1_sb", [P, TOP1 // P])
        wt2_sb = sb("wt2_sb", [P, TOP1 // P, TOP2])
        bt2_sb = sb("bt2_sb", [P, TOP2 // P])
        wt3_sb = sb("wt3_sb", [P, TOP2 // P])
        y_sb = sb("y_sb", [1, B])
        w1_raw = prod[:, 0, :, :]
        w0a_sb = prod[:, 1, 0:KP, :]
        w0b_sb = prod[:, 1, KP:2 * KP, :]
        a1 = z[:, 0:4, :]
        a2 = second[:, 0:2, :]

        ps_y = ctx.enter_context(nc.psum_tensor("ps_y", [P, RING, BANK], F32))
        ps_c = ctx.enter_context(nc.psum_tensor("ps_c", [P, COLS], F32))
        ps_h1 = ctx.enter_context(nc.psum_tensor("ps_h1", [P, B], F32))

        ids_in = sem("ids_in")
        w0_in = sem("w0_in")
        w1_in = sem("w1_in")
        top_in = sem("top_in")
        rows_step = sem("rows_step")
        w_ready = sem("w_ready")
        w1_hi_ready = sem("w1_hi_ready")
        w0_step = sem("w0_step")
        ones_zeroed = sem("ones_zeroed")
        rows_staged = sem("rows_staged")
        pool_passed = sem("pool_passed")
        sp_passed = sem("sp_passed")
        gathered = [sem(f"gathered{s}") for s in range(SLOTS)]
        et_written = sem("et_written")
        pairs_in = sem("pairs_in")
        es_ready = sem("es_ready")
        z_ready = sem("z_ready")
        z_hi_ready = sem("z_hi_ready")
        z_lo_ready = sem("z_lo_ready")
        l0_done = sem("l0_done")
        c_ready = sem("c_ready")
        c_hi_ready = sem("c_hi_ready")
        c_lo_ready = sem("c_lo_ready")
        h0_done = sem("h0_done")
        y_ready = sem("y_ready")
        act_scaled = sem("act_scaled")
        dve_scaled = sem("dve_scaled")
        added = sem("added")
        reduced = sem("reduced")
        c1_ready = sem("c1_ready")
        h1_done = sem("h1_done")
        h1_copied = sem("h1_copied")
        mm_top = sem("mm_top")
        act_top = sem("act_top")
        y_out = sem("y_out")

        block = ctx.enter_context(nc.Block())

        def buffer_of(g, u):
            return (TG * g.r + u) % BUFS

        def before(g, u, n=1):
            return (g, u - n) if u >= n else (g.plus(-1), u + TG - n)

        def bank_of(g, u, k):
            return (NK * (TG * g.r + u) + k) % RING

        @block.sync
        def _(sp):
            sp.dma_start(ids_sb[:, :], ids).then_inc(ids_in, 16)
            sp.dma_start(base_sb[:, :], row_base).then_inc(ids_in, 16)
            sp.dma_start(last_sb[:, :], row_last).then_inc(ids_in, 16)
            sp.dma_start(w0a_sb, w0a).then_inc(w0_in, 16)
            sp.dma_start(w0b_sb, w0b).then_inc(w0_in, 16)
            sp.dma_start(w1_raw, w1.rearrange("(h m) n -> m h n", m=N)).then_inc(w1_in, 16)

            def pairs(g):
                cols = g.times(COLS)
                sp.wait_ge(gathered[g.r], g.uses(16 * TG))
                sp.sem_inc(sp_passed, 1)
                for b in range(BT):
                    here = et.rearrange("(two f) c -> f two c", two=2)[:, :, bass.ds(cols + b * TG * D, TG * D)]
                    src = gat[b * F:(b + 1) * F, g.r, :].unsqueeze(1).to_broadcast([F, 2, TG * D])
                    sp.dma_start(here, src).then_inc(et_written, 16)
                sp.wait_ge(et_written, g.times(16 * BT, 16 * BT))
                sp.sem_inc(sp_passed, 1)
                wait(sp, z_ready, g.times(KP))
                sp.sem_inc(sp_passed, 1)
                row = B * D
                lead = et[0:1, bass.ds(cols, COLS)]

                def shifted(rows_on, step):
                    return bass.AP(tensor=lead.tensor, offset=lead.offset + rows_on * row,
                                   ap=[[row, F], [step, SH], [1, COLS]])

                sp.dma_start(first[:, :], shifted(0, 0)).then_inc(pairs_in, 16)
                for k in range(KP):
                    sp.dma_start(second[:, k, :], shifted(SH * k, row)).then_inc(pairs_in, 16)

            for g in range(SLOTS):
                pairs(Group(0, g))
            sp.dma_start(wt1_sb[:, :, :], wt1[0:2 * P, :].rearrange("(k p) n -> p k n", p=P)).then_inc(top_in, 16)
            sp.dma_start(wt1_d[:, :], wt1[2 * P:2 * P + DENSE, :]).then_inc(top_in, 16)
            sp.dma_start(wt2_sb[:, :, :], wt2.rearrange("(k p) n -> p k n", p=P)).then_inc(top_in, 16)
            sp.dma_start(wt3_sb[:, :], wt3).then_inc(top_in, 16)
            sp.dma_start(bt1_sb[:, :], bt1).then_inc(top_in, 16)
            sp.dma_start(bt2_sb[:, :], bt2).then_inc(top_in, 16)
            sp.dma_start(hd[:, :], dense_t).then_inc(top_in, 16)

            def body(g, number):
                if number is None or number + SLOTS < GROUPS:
                    pairs(g.plus(SLOTS))

            over_groups(sp, body)
            sp.wait_ge(act_top, 7)
            sp.dma_start(y, y_sb[:, :]).then_inc(y_out, 16)
            sp.wait_ge(y_out, 16)

        @block.gpsimd
        def _(pool):
            def gather(g, tiles):
                if 0 in tiles:
                    stage(g)
                for u in tiles:
                    pool.indirect_dma_start(
                        out=gat[:, g.r, u * D:(u + 1) * D], out_offset=None, in_=table,
                        in_offset=bass.IndirectOffsetOnAxis(ap=rows_now[:, g.r, u:u + 1], axis=0),
                    ).then_inc(gathered[g.r], 16)

            def stage(g):
                if not isinstance(g.i, int) or g.i > 0:
                    pool.wait_ge(es_ready, g.times(1, 1 - SLOTS))
                    pool.wait_ge(et_written, g.times(16 * BT, 16 * BT * (1 - SLOTS)))
                nc.gpsimd.tensor_copy(rows_now[:, g.r, :], rows[:, bass.ds(g.times(TG), TG)]).then_inc(rows_staged, 1)
                pool.wait_ge(rows_staged, g.times(1, 1))
                pool.sem_inc(pool_passed, 1)

            def split_z(g, k):
                pool.wait_ge(z_hi_ready, g.times(KS, k + 1))
                wait(pool, l0_done, g.times(1))
                nc.gpsimd.tensor_tensor(z_lo[:, k, :], z[:, k, :], z_hi[:, k, :].bitcast(F32),
                                        ALU.subtract).then_inc(z_lo_ready, 1)

            def add(g, u):
                pool.wait_ge(act_scaled, signals(ACT_BANKS, g, u, ADD_AFTER))
                pool.wait_ge(dve_scaled, signals(DVE_BANKS, g, u, ADD_AFTER))
                buf = buffer_of(g, u)
                low, high = prod[:, buf, 0:ADD, :], prod[:, buf, ADD:2 * ADD, :]
                nc.gpsimd.tensor_tensor(high, high, low, ALU.add).then_inc(added, 1)

            pool.wait_ge(rows_step, 5)
            for g in range(SLOTS):
                gather(Group(0, g), range(TG))

            def body(g, number):
                for u in range(TG):
                    if not (number == 0 and u == 0):
                        add(*before(g, u))
                    if u < 2 and (number is None or number + 1 < GROUPS):
                        split_z(g.plus(1), 2 * u)
                        split_z(g.plus(1), 2 * u + 1)
                    if u >= 2 and (number is None or number + SLOTS < GROUPS):
                        gather(g.plus(SLOTS), ((0, 1), (2, 3))[u - 2])

            over_groups(pool, body)
            add(LAST, TG - 1)

        @block.scalar
        def _(act):
            def split_z(g, k):
                act.wait_ge(z_ready, g.times(KP, k + 1))
                wait(act, l0_done, g.times(1))
                nc.scalar.activation(z_hi[:, k, :], z[:, k, :], ACT.Copy).then_inc(z_hi_ready, 1)

            def rectify(g):
                act.wait_ge(l0_done, g.times(1, 1))
                wait(act, h0_done, g.times(1))
                nc.scalar.activation(c[:, :], ps_c[:, :], ACT.Relu).then_inc(c_ready, 1)
                nc.scalar.activation(
                    c_hi[:, g.r, :].rearrange("p (u b d) -> p b u d", u=TG, b=BT),
                    ps_c[:, :].rearrange("p (b u d) -> p b u d", u=TG, b=BT), ACT.Relu,
                ).then_inc(c_hi_ready, 1)

            def scale(g, u, k):
                if k == ACT_BANKS[u][0]:
                    if u == 0:
                        act.wait_ge(es_ready, g.times(1, 1))
                    wait(act, reduced, g.times(TG * HALVES, (u + 1 - BUFS) * HALVES))
                act.wait_ge(y_ready, g.times(TG * NK, u * NK + k + 1))
                for j in range(HB):
                    h = HB * k + j
                    last = nc.scalar.activation(prod[:, buffer_of(g, u), h, :],
                                                ps_y[:, bank_of(g, u, k), j * N:(j + 1) * N], ACT.Copy,
                                                scale=es[:, g.r, u, h:h + 1])
                last.then_inc(act_scaled, 1)

            act.wait_ge(w1_in, 16)
            for k in range(NK):
                nc.scalar.activation(w1_hi[:, k * HB:(k + 1) * HB, :], w1_raw[:, k * HB:(k + 1) * HB, :],
                                     ACT.Copy).then_inc(w1_hi_ready, 1)
            for k in range(KS):
                split_z(Group(0, 0), k)
            rectify(Group(0, 0))
            for k in (0, 1):
                split_z(Group(0, 1), k)
            act.wait_ge(w_ready, 2)

            def body(g, number):
                more = number is None or number + 1 < GROUPS
                for u in range(TG):
                    for k in range(NK):
                        if k in ACT_BANKS[u]:
                            scale(g, u, k)
                        for (n, chunk), at in Z_HI_AT.items():
                            if at == (u, k) and (number is None or number + n < GROUPS):
                                split_z(g.plus(n), chunk)
                        if more and (u, k) == (3, 1):
                            rectify(g.plus(1))

            Z_HI_AT = {(2, 0): (3, 4), (2, 1): (3, 7), (1, 2): (0, 2), (1, 3): (0, 5)}
            over_groups(act, body)

            act.wait_ge(h1_done, TILES)
            nc.scalar.activation(h1[:, :], ps_h1[:, :], ACT.Copy).then_inc(h1_copied, 1)
            act.wait_ge(top_in, 7 * 16)
            for j in range(TOP1 // P):
                act.wait_ge(mm_top, j + 1)
                nc.scalar.activation(a1[:, j, :], ps_y[:, j, :], ACT.Relu, bias=bt1_sb[:, j:j + 1]).then_inc(act_top, 1)
            for j in range(TOP2 // P):
                act.wait_ge(mm_top, 5 + j)
                nc.scalar.activation(a2[:, j, :], ps_y[:, 4 + j, :], ACT.Relu, bias=bt2_sb[:, j:j + 1]).then_inc(act_top, 1)
            act.wait_ge(mm_top, 7)
            nc.scalar.activation(y_sb[:, :], ps_c[0:1, :], ACT.Copy).then_inc(act_top, 1)

        @block.vector
        def _(dve):
            dve.wait_ge(ids_in, 48)
            nc.vector.tensor_copy(idf[:, :], ids_sb[:, :]).then_inc(rows_step, 1)
            dve.wait_ge(rows_step, 1)
            nc.vector.tensor_scalar(neg[:, :], idf[:, :], 0.0, last_sb[:, 1:2], ALU.is_lt, ALU.mult).then_inc(rows_step, 1)
            dve.wait_ge(rows_step, 2)
            nc.vector.tensor_tensor(idf[:, :], idf[:, :], neg[:, :], ALU.add).then_inc(rows_step, 1)
            dve.wait_ge(rows_step, 3)
            nc.vector.tensor_scalar(neg[:, :], idf[:, :], 0.0, last_sb[:, 0:1], ALU.max, ALU.min).then_inc(rows_step, 1)
            dve.wait_ge(rows_step, 4)
            nc.vector.tensor_scalar(rows[:, :], neg[:, :], base_sb[:, 0:1], None, ALU.add).then_inc(rows_step, 1)

            nc.vector.memset(ones_b[:, :], 0.0).then_inc(ones_zeroed, 1)
            dve.wait_ge(ones_zeroed, 1)
            for b in range(BT):
                nc.vector.memset(ones_b[b * D:(b + 1) * D, b:b + 1], 1.0).then_inc(ones_zeroed, 1)

            dve.wait_ge(w0_in, 32)
            nc.vector.tensor_tensor(w0_sum[:, :, :], w0a_sb, w0b_sb, ALU.add).then_inc(w0_step, 1)
            dve.wait_ge(w0_step, 1)
            nc.vector.tensor_copy(w0_hi[:, :, :], w0_sum[:, 0:KS, :]).then_inc(w0_step, 1)
            dve.wait_ge(w0_step, 2)
            nc.vector.tensor_tensor(w0_lo[:, :, :], w0_sum[:, 0:KS, :], w0_hi[:, :, :].bitcast(F32), ALU.subtract).then_inc(w_ready, 1)

            def turn(g):
                dve.wait_ge(gathered[g.r], g.uses(16 * TG))
                nc.vector.transpose(es[:, g.r, :, :].rearrange("p u f -> p (u f)"), gat[:, g.r, :]).then_inc(es_ready, 1)

            def multiply(g, k):
                if k == 0:
                    dve.wait_ge(pairs_in, g.times(16 * (KP + 1), 16 * (KP + 1)))
                if k < KS:
                    wait(dve, z_lo_ready, g.times(KS, k + 1 - KS))
                else:
                    wait(dve, l0_done, g.times(1))
                nc.vector.tensor_tensor(z[:, k, :], first[:, :], second[:, k, :], ALU.mult).then_inc(z_ready, 1)

            def split_c(g):
                dve.wait_ge(c_hi_ready, g.times(1, 1))
                nc.vector.tensor_tensor(
                    c_lo[:, g.r, :].rearrange("p (u b d) -> p b u d", u=TG, b=BT),
                    c[:, :].rearrange("p (b u d) -> p b u d", u=TG, b=BT),
                    c_hi[:, g.r, :].bitcast(F32).rearrange("p (u b d) -> p b u d", u=TG, b=BT),
                    ALU.subtract).then_inc(c_lo_ready, 1)

            def sum_h0(g):
                nc.vector.tensor_reduce(
                    h0[:, bass.ds(g.times(TG * BT), TG * BT)].rearrange("p (u b) -> p b u", u=TG),
                    c[:, :].rearrange("p (b u d) -> p b u d", u=TG, b=BT), AX.X, ALU.add).then_inc(h0_done, 1)

            def scale(g, u, k):
                if k == DVE_BANKS[u][0]:
                    if u == 0:
                        dve.wait_ge(es_ready, g.times(1, 1))
                    wait(dve, reduced, g.times(TG * HALVES, (u + 1 - BUFS) * HALVES))
                dve.wait_ge(y_ready, g.times(TG * NK, u * NK + k + 1))
                fields = slice(HB * k, HB * (k + 1))
                nc.vector.tensor_tensor(
                    prod[:, buffer_of(g, u), fields, :],
                    ps_y[:, bank_of(g, u, k), :].rearrange("p (h n) -> p h n", n=N),
                    es[:, g.r, u, fields].unsqueeze(2).to_broadcast([P, HB, N]), ALU.mult).then_inc(dve_scaled, 1)

            def reduce(g, u, half):
                if half == 0:
                    dve.wait_ge(added, g.times(TG, u + 1))
                    dve.wait_ge(act_scaled, signals(ACT_BANKS, g, u, NK - 1))
                    dve.wait_ge(dve_scaled, signals(DVE_BANKS, g, u, NK - 1))
                    wait(dve, c1_ready, g.times(TG, u))
                maps = slice(half * N // HALVES, (half + 1) * N // HALVES)
                nc.vector.tensor_reduce(csum[:, maps], prod[:, buffer_of(g, u), ADD:F, maps].rearrange("p h n -> p n h"),
                                        AX.X, ALU.add).then_inc(reduced, 1)

            def rectify(g, u):
                dve.wait_ge(reduced, g.times(TG * HALVES, (u + 1) * HALVES))
                wait(dve, h1_done, g.times(TG, u - 1))
                nc.vector.tensor_scalar(c1[:, u % 2, :], csum[:, :], 0.0, None, ALU.max).then_inc(c1_ready, 1)

            for k in range(NK):
                dve.wait_ge(w1_hi_ready, k + 1)
                part = slice(k * HB, (k + 1) * HB)
                last = nc.vector.tensor_tensor(w1_lo[:, part, :], w1_raw[:, part, :],
                                               w1_hi[:, part, :].bitcast(F32), ALU.subtract)
            last.then_inc(w_ready, 1)
            turn(Group(0, 0))
            for k in range(KP):
                multiply(Group(0, 0), k)
            for k in range(KS):
                dve.wait_ge(z_hi_ready, k + 1)
                nc.vector.tensor_tensor(z_lo[:, k, :], z[:, k, :], z_hi[:, k, :].bitcast(F32),
                                        ALU.subtract).then_inc(z_lo_ready, 1)
            split_c(Group(0, 0))
            sum_h0(Group(0, 0))
            for k in (0, 1):
                multiply(Group(0, 1), k)
            dve.wait_ge(w_ready, 2)

            Z_AT = {(2, 0): (3, 0), (2, 1): (3, 3), (1, 2): (0, 0), (1, 3): (0, 3), (1, 4): (1, 3)}

            def body(g, number):
                more = number is None or number + 1 < GROUPS
                for u in range(TG):
                    for k in range(NK):
                        if k in DVE_BANKS[u]:
                            scale(g, u, k)
                        if k == 2 and not (number == 0 and u < 2):
                            reduce(*before(g, u, 2), 1)
                        if k == 4 and not (number == 0 and u < 2):
                            rectify(*before(g, u, 2))
                        if k == 6 and not (number == 0 and u == 0):
                            reduce(*before(g, u), 0)
                        for (n, chunk), at in Z_AT.items():
                            if at == (u, k) and (number is None or number + n < GROUPS):
                                multiply(g.plus(n), chunk)
                        if more and (u, k) == (2, 3):
                            turn(g.plus(1))
                        if more and (u, k) == (3, 3):
                            split_c(g.plus(1))
                        if more and (u, k) == (3, 5):
                            sum_h0(g.plus(1))

            over_groups(dve, body)
            reduce(LAST, TG - 2, 1)
            rectify(LAST, TG - 2)
            for half in range(HALVES):
                reduce(LAST, TG - 1, half)
            rectify(LAST, TG - 1)

        @block.tensor
        def _(pe):
            def layer0(g, k):
                if k == 0:
                    wait(pe, c_hi_ready, g.times(1))
                if k == KS:
                    pe.wait_ge(z_ready, g.times(KP, KP))
                    nc.tensor.matmul(ps_c[:, :], w0_sum[:, k, :], z[:, k, :], start=False, stop=True).then_inc(l0_done, 1)
                    return
                pe.wait_ge(z_hi_ready, g.times(KS, k + 1))
                pe.wait_ge(z_lo_ready, g.times(KS, k + 1))
                nc.tensor.matmul(ps_c[:, :], w0_hi[:, k, :], z_hi[:, k, :], start=(k == 0), stop=False)
                nc.tensor.matmul(ps_c[:, :], w0_lo[:, k, :], z_hi[:, k, :], start=False, stop=False)
                nc.tensor.matmul(ps_c[:, :], w0_hi[:, k, :], z_lo[:, k, :], start=False, stop=False)

            def layer1(g, u, k, number):
                if number is None or number > 0 or NK * u + k >= RING:
                    wait(pe, act_scaled, signals(ACT_BANKS, g, u, k - RING))
                    wait(pe, dve_scaled, signals(DVE_BANKS, g, u, k - RING))
                out = ps_y[:, bank_of(g, u, k), :]
                hi, lo = (x[:, g.r, u * P:(u + 1) * P] for x in (c_hi, c_lo))
                w_hi, w_lo = (x[:, k * HB:(k + 1) * HB, :].rearrange("p h n -> p (h n)") for x in (w1_hi, w1_lo))
                nc.tensor.matmul(out, hi, w_hi, start=True, stop=False)
                nc.tensor.matmul(out, hi, w_lo, start=False, stop=False)
                nc.tensor.matmul(out, lo, w_hi, start=False, stop=True).then_inc(y_ready, 1)

            def sum_h1(g, u):
                pe.wait_ge(c1_ready, g.times(TG, u + 1))
                nc.tensor.matmul(ps_h1[:, bass.ds(g.times(TG * BT, u * BT), BT)], c1[:, u % 2, :], ones_b[:, :],
                                 start=True, stop=True).then_inc(h1_done, 1)

            pe.wait_ge(ones_zeroed, 1 + BT)
            pe.wait_ge(w_ready, 1)
            for k in range(KP):
                layer0(Group(0, 0), k)
            pe.wait_ge(w_ready, 2)

            Z_USED_AT = ((1, 1), (1, 4), (2, 1), (2, 4), (2, 6))

            def body(g, number):
                more = number is None or number + 1 < GROUPS
                pe.wait_ge(c_hi_ready, g.times(1, 1))
                pe.wait_ge(c_lo_ready, g.times(1, 1))
                for u in range(TG):
                    for k in range(NK):
                        layer1(g, u, k, number)
                        if more and (u, k) in Z_USED_AT:
                            layer0(g.plus(1), Z_USED_AT.index((u, k)))
                        if k == 3 and not (number == 0 and u < 3):
                            sum_h1(*before(g, u, 3))

            over_groups(pe, body)
            sum_h1(LAST, TG - 3)
            sum_h1(LAST, TG - 2)
            sum_h1(LAST, TG - 1)

            pe.wait_ge(top_in, 7 * 16)
            pe.wait_ge(h0_done, GROUPS)
            pe.wait_ge(h1_copied, 1)
            for j in range(TOP1 // P):
                cols = slice(j * P, (j + 1) * P)
                nc.tensor.matmul(ps_y[:, j, :], wt1_sb[:, 0, cols], h0[:, :], start=True, stop=False)
                nc.tensor.matmul(ps_y[:, j, :], wt1_d[:, cols], hd[:, :], start=False, stop=False)
                nc.tensor.matmul(ps_y[:, j, :], wt1_sb[:, 1, cols], h1[:, :], start=False, stop=True).then_inc(mm_top, 1)
            for k in range(TOP1 // P):
                pe.wait_ge(act_top, k + 1)
                for j in range(TOP2 // P):
                    last = nc.tensor.matmul(ps_y[:, 4 + j, :], wt2_sb[:, k, j * P:(j + 1) * P], a1[:, k, :],
                                            start=(k == 0), stop=(k == TOP1 // P - 1))
                    if k == TOP1 // P - 1:
                        last.then_inc(mm_top, 1)
            for k in range(TOP2 // P):
                pe.wait_ge(act_top, TOP1 // P + k + 1)
                last = nc.tensor.matmul(ps_c[0:1, :], wt3_sb[:, k:k + 1], a2[:, k, :],
                                        start=(k == 0), stop=(k == TOP2 // P - 1))
            last.then_inc(mm_top, 1)


def pair_rows():
    a = np.full((F, SH, KP), F * F)
    b = np.full((F, SH, KP), F * F)
    for k in range(KP):
        for s in range(SH):
            dist = SH * k + s
            for h in range(F):
                m = (h + dist) % F
                if dist < F // 2 or (dist == F // 2 and h < F // 2):
                    a[h, s, k] = F * h + m
                    if dist:
                        b[h, s, k] = F * m + h
    return a.reshape(P, KP), b.reshape(P, KP)


def kernel(**inputs):
    import concourse.bacc as bacc
    from concourse.bass_utils import run_bass_kernel_spmd

    x = {name: np.asarray(a) for name, a in inputs.items()}
    tables = [x[f"tbl_{f}"] for f in range(F)]
    counts = np.array([t.shape[0] for t in tables])
    bases = np.cumsum(counts) - counts
    rows_a, rows_b = pair_rows()
    w0 = np.concatenate([x["L0_rec_filter_0"][0], np.zeros((1, N), np.float32)])
    arrays = {
        "ids": np.ascontiguousarray(x["ids"].reshape(TILES, BT, F).transpose(1, 2, 0).reshape(P, TILES)),
        "row_base": np.tile(bases.astype(np.float32), BT).reshape(P, 1),
        "row_last": np.tile(np.stack([counts - 1, counts], 1).astype(np.float32), (BT, 1)),
        "table": np.concatenate(tables),
        "dense_t": np.ascontiguousarray(x["dense_ctx"].T),
        "w0a": w0[rows_a],
        "w0b": w0[rows_b],
        "w1": np.ascontiguousarray(x["L0_rec_filter_1"][0]),
        "wt1": x["W_top1"],
        "bt1": np.ascontiguousarray(x["b_top1"].reshape(TOP1 // P, P).T),
        "wt2": x["W_top2"],
        "bt2": np.ascontiguousarray(x["b_top2"].reshape(TOP2 // P, P).T),
        "wt3": np.ascontiguousarray(x["W_top3"].reshape(TOP2 // P, P).T),
    }
    nc = bacc.Bacc("TRN2", target_bir_lowering=False, num_devices=1)
    args = [nc.dram_tensor(n, a.shape, mybir.dt.from_np(a.dtype), kind="ExternalInput").ap() for n, a in arrays.items()]
    y = nc.dram_tensor("y", (1, B), F32, kind="ExternalOutput").ap()
    tower(nc, *args, y)
    r = run_bass_kernel_spmd(nc, [arrays], core_ids=[0])
    return r.results[0]["y"].reshape(B, 1)
```

```python
from contextlib import ExitStack

import numpy as np

import concourse.bass as bass
from concourse import mybir

F32 = mybir.dt.float32
F32R = mybir.dt.float32r
I32 = mybir.dt.int32
U32 = mybir.dt.uint32
ALU = mybir.AluOpType
ACT = mybir.ActivationFunctionType
AX = mybir.AxisListType

B, F, D, N, DENSE = 512, 32, 32, 128, 16
TOP1, TOP2 = 512, 256
P = 128
BT = P // D
TILES = B // BT
TG = 4
GROUPS = TILES // TG
COLS = TG * P
KP = 5
SH = P // F
BANK = 512
HB = BANK // N
NK = F // HB
RING = 6
SLOTS = 3
BUFS = 3
LASTK = KP - 1
WARM_UP = 22
W1_LOADS = 4
ACT_BANKS = ((0, 1, 3, 5, 6),) * TG
DVE_BANKS = tuple(tuple(k for k in range(NK) if k not in a) for a in ACT_BANKS)
ADD = 12
ADDS_LAST = ((0, 8), (8, 12))
HALVES = 2


def signals(banks, g, u, k):
    if k < 0:
        g, u, k = (g, u - 1, k + NK) if u else (g.plus(-1), TG - 1, k + NK)
    return g.times(sum(map(len, banks)), sum(map(len, banks[:u])) + sum(x <= k for x in banks[u]))


class Group:

    def __init__(self, i, r):
        self.i, self.r = (i if 0 <= r < SLOTS else i + r // SLOTS), r % SLOTS

    def plus(self, n):
        return Group(self.i, self.r + n)

    def times(self, k, add=0):
        return self.i * (SLOTS * k) + (self.r * k + add)

    def uses(self, k):
        return self.i * k + k


def wait(engine, semaphore, value):
    if not isinstance(value, int) or value > 0:
        engine.wait_ge(semaphore, value)


def over_groups(engine, body):
    body(Group(0, 0), 0)
    body(Group(0, 1), 1)
    loops = (GROUPS - 2) // SLOTS - 1
    with engine.Fori(0, loops) as i:
        for r in range(2, 2 + SLOTS):
            body(Group(i, r), None)
    for g in range(2 + SLOTS * loops, GROUPS):
        body(Group(g // SLOTS, g % SLOTS), g)


LAST = Group((GROUPS - 1) // SLOTS, (GROUPS - 1) % SLOTS)


def tower(nc, ids, bounds, copy_of, table, dense_t, w0a, w0b, w1, wt1, bt1, wt2, bt2, wt3, y):
    ctx = ExitStack()
    with ctx:
        def sb(name, shape, dt=F32):
            return ctx.enter_context(nc.sbuf_tensor(name, shape, dt))

        def sem(name):
            return ctx.enter_context(nc.semaphore(name))

        et = nc.dram_tensor("et_scratch", [2 * F, B * D], F32, kind="Internal").ap()

        ids_sb = sb("ids_sb", [P, TILES], I32)
        idf = sb("idf", [P, TILES])
        neg = sb("neg", [P, TILES])
        bounds_sb = sb("bounds_sb", [P, 3])
        rows = sb("rows", [P, TILES], U32)
        rows_now = sb("rows_now", [P, SLOTS, TG], U32)
        gat = sb("gat", [P, SLOTS, TG * D])
        es = sb("es", [P, SLOTS, TG, F])
        first = sb("first", [P, COLS])
        second = sb("second", [P, KP, COLS])
        z = sb("z", [P, KP, COLS])
        z_hi = sb("z_hi", [P, KP, COLS], F32R)
        z_lo = sb("z_lo", [P, KP, COLS], F32R)
        copy_sb = sb("copy_sb", [P, 2])
        c = sb("c", [P, COLS])
        c_hi = sb("c_hi", [P, SLOTS, COLS], F32R)
        c_lo = sb("c_lo", [P, SLOTS, COLS], F32R)
        w0_sum = sb("w0_sum", [P, KP, N])
        w0_hi = sb("w0_hi", [P, KP, N], F32R)
        w0_lo = sb("w0_lo", [P, KP, N], F32R)
        w1_hi = sb("w1_hi", [P, F, N], F32R)
        w1_lo = sb("w1_lo", [P, F, N], F32R)
        prod = sb("prod", [P, BUFS, F, N])
        csum = sb("csum", [P, N])
        c1 = sb("c1", [P, 2, N])
        ones_b = sb("ones_b", [P, BT])
        h0 = sb("h0", [P, B])
        hd = sb("hd", [DENSE, B])
        wt1_sb = sb("wt1_sb", [P, 2, TOP1])
        wt1_d = sb("wt1_d", [DENSE, TOP1])
        bt1_sb = sb("bt1_sb", [P, TOP1 // P])
        wt2_sb = sb("wt2_sb", [P, TOP1 // P, TOP2])
        bt2_sb = sb("bt2_sb", [P, TOP2 // P])
        wt3_sb = sb("wt3_sb", [P, TOP2 // P])
        y_sb = sb("y_sb", [1, B])
        w1_raw = prod[:, 0, :, :]
        w0a_sb = prod[:, 1, 0:KP, :]
        w0b_sb = prod[:, 1, KP:2 * KP, :]
        a1 = z[:, 0:4, :]
        a1_hi, a1_lo = (x[:, 0:TOP1 // P * HB, :].rearrange("p (k h) n -> p k (h n)", h=HB) for x in (w1_hi, w1_lo))
        a2 = second[:, 0:2, :]
        wt2_hi, wt2_lo = (x[:, 0:2, :].rearrange("p a (k n) -> p (a k) n", n=TOP2) for x in (z_hi, z_lo))
        wt1_hi, wt1_lo = z_hi[:, 2, :], z_lo[:, 2, :]
        h1_hi, h1_lo = z_hi[:, 3, :], z_lo[:, 3, :]

        ps_y = ctx.enter_context(nc.psum_tensor("ps_y", [P, RING, BANK], F32))
        ps_c = ctx.enter_context(nc.psum_tensor("ps_c", [P, COLS], F32))
        ps_h1 = ctx.enter_context(nc.psum_tensor("ps_h1", [P, B], F32))

        ids_in = sem("ids_in")
        w0_in = sem("w0_in")
        w1_in = [sem(f"w1_in{n}") for n in range(W1_LOADS)]
        top_in = sem("top_in")
        rows_step = sem("rows_step")
        w_ready = sem("w_ready")
        w1_hi_ready = sem("w1_hi_ready")
        w0_step = sem("w0_step")
        ones_zeroed = sem("ones_zeroed")
        rows_staged = sem("rows_staged")
        pool_passed = sem("pool_passed")
        sp_passed = sem("sp_passed")
        gathered = [sem(f"gathered{s}") for s in range(SLOTS)]
        et_written = sem("et_written")
        pairs_in = [sem(f"pairs_in{k}") for k in range(KP)]
        es_ready = sem("es_ready")
        z_ready = sem("z_ready")
        z_hi_ready = sem("z_hi_ready")
        z_lo_ready = sem("z_lo_ready")
        first_odd_z_lo = sem("first_odd_z_lo")
        l0_done = sem("l0_done")
        c_ready = sem("c_ready")
        c_hi_ready = sem("c_hi_ready")
        c_lo_ready = sem("c_lo_ready")
        first_c_hi = sem("first_c_hi")
        first_c = sem("first_c")
        first_c_lo = sem("first_c_lo")
        h0_done = sem("h0_done")
        y_ready = sem("y_ready")
        act_scaled = sem("act_scaled")
        dve_scaled = sem("dve_scaled")
        added = sem("added")
        reduced = sem("reduced")
        c1_ready = sem("c1_ready")
        h1_done = sem("h1_done")
        h1_hi_ready = sem("h1_hi_ready")
        h1_lo_ready = sem("h1_lo_ready")
        top_hi_ready = sem("top_hi_ready")
        top_lo_ready = sem("top_lo_ready")
        a1_hi_ready = sem("a1_hi_ready")
        a1_ready = sem("a1_ready")
        a1_lo_ready = sem("a1_lo_ready")
        mm_top = sem("mm_top")
        act_top = sem("act_top")
        y_out = sem("y_out")

        block = ctx.enter_context(nc.Block())

        def buffer_of(g, u):
            return (TG * g.r + u) % BUFS

        def before(g, u, n=1):
            return (g, u - n) if u >= n else (g.plus(-1), u + TG - n)

        def bank_of(g, u, k):
            return (NK * (TG * g.r + u) + k) % RING

        free = [ps_y[:, bank_of(LAST, TG - 1, k), :] for k in range(NK - RING, NK)]
        ps_a1, ps_a2 = free[:TOP1 // P], free[TOP1 // P:]

        @block.sync
        def _(sp):
            sp.dma_start(ids_sb[:, :], ids).then_inc(ids_in, 16)
            sp.dma_start(bounds_sb[:, :], bounds).then_inc(ids_in, 16)
            sp.dma_start(w0a_sb, w0a).then_inc(w0_in, 16)
            sp.dma_start(w0b_sb, w0b).then_inc(w0_in, 16)
            sp.dma_start(copy_sb[:, :], copy_of).then_inc(w0_in, 16)
            for n in range(W1_LOADS):
                fields = slice(n * F // W1_LOADS, (n + 1) * F // W1_LOADS)
                sp.dma_start(w1_raw[:, fields, :], w1.rearrange("(h m) n -> m h n", m=N)[:, fields, :]).then_inc(w1_in[n], 16)

            def pairs(g):
                cols = g.times(COLS)
                sp.wait_ge(gathered[g.r], g.uses(16 * TG))
                sp.sem_inc(sp_passed, 1)
                for copy in range(2):
                    here = et[copy * F:(copy + 1) * F, bass.ds(cols, COLS)].rearrange("f (b c) -> b f c", b=BT)
                    sp.dma_start(here, gat[:, g.r, :]).then_inc(et_written, 16)
                sp.wait_ge(et_written, g.times(32, 32))
                sp.sem_inc(sp_passed, 1)
                wait(sp, z_ready, g.times(KP))
                sp.sem_inc(sp_passed, 1)
                row = B * D
                lead = et[0:1, bass.ds(cols, COLS)]

                def shifted(rows_on, step):
                    return bass.AP(tensor=lead.tensor, offset=lead.offset + rows_on * row,
                                   ap=[[row, F], [step, SH], [1, COLS]])

                sp.dma_start(first[:, :], shifted(0, 0)).then_inc(pairs_in[0], 16)
                for k in range(KP):
                    sp.dma_start(second[:, k, :], shifted(SH * k, row if k < LASTK else 0)).then_inc(pairs_in[k], 16)

            pairs(Group(0, 0))
            for g in range(1, SLOTS):
                pairs(Group(0, g))
            sp.dma_start(wt1_sb[:, :, :], wt1[0:2 * P, :].rearrange("(k p) n -> p k n", p=P)).then_inc(top_in, 16)
            sp.dma_start(wt1_d[:, :], wt1[2 * P:2 * P + DENSE, :]).then_inc(top_in, 16)
            sp.dma_start(wt2_sb[:, :, :], wt2.rearrange("(k p) n -> p k n", p=P)).then_inc(top_in, 16)
            sp.dma_start(wt3_sb[:, :], wt3).then_inc(top_in, 16)
            sp.dma_start(bt1_sb[:, :], bt1).then_inc(top_in, 16)
            sp.dma_start(bt2_sb[:, :], bt2).then_inc(top_in, 16)
            sp.dma_start(hd[:, :], dense_t).then_inc(top_in, 16)

            def body(g, number):
                if number is None or number + SLOTS < GROUPS:
                    pairs(g.plus(SLOTS))

            over_groups(sp, body)
            sp.wait_ge(act_top, 3)
            sp.dma_start(y, y_sb[:, :]).then_inc(y_out, 16)
            sp.wait_ge(y_out, 16)

        @block.gpsimd
        def _(pool):
            def gather(g, tiles):
                if 0 in tiles:
                    stage(g)
                for u in tiles:
                    pool.indirect_dma_start(
                        out=gat[:, g.r, u * D:(u + 1) * D], out_offset=None, in_=table,
                        in_offset=bass.IndirectOffsetOnAxis(ap=rows_now[:, g.r, u:u + 1], axis=0),
                    ).then_inc(gathered[g.r], 16)

            def stage(g):
                if not isinstance(g.i, int) or g.i > 0:
                    pool.wait_ge(es_ready, g.times(1, 1 - SLOTS))
                    pool.wait_ge(et_written, g.times(32, 32 * (1 - SLOTS)))
                nc.gpsimd.tensor_copy(rows_now[:, g.r, :], rows[:, bass.ds(g.times(TG), TG)]).then_inc(rows_staged, 1)
                pool.wait_ge(rows_staged, g.times(1, 1))
                pool.sem_inc(pool_passed, 1)

            def split_z(g, k):
                pool.wait_ge(z_hi_ready, g.times(KP, k + 1))
                wait(pool, l0_done, g.times(1))
                nc.gpsimd.tensor_tensor(z_lo[:, k, :], z[:, k, :], z_hi[:, k, :].bitcast(F32),
                                        ALU.subtract).then_inc(z_lo_ready, 1)

            def add(g, u, start=0, end=ADD):
                last_bank = (2 * end - start - 1) // HB
                pool.wait_ge(act_scaled, signals(ACT_BANKS, g, u, last_bank))
                pool.wait_ge(dve_scaled, signals(DVE_BANKS, g, u, last_bank))
                buf = buffer_of(g, u)
                low, high = prod[:, buf, start:end, :], prod[:, buf, end:2 * end - start, :]
                nc.gpsimd.tensor_tensor(high, high, low, ALU.add).then_inc(added, 1)

            pool.wait_ge(rows_step, 5)
            for g in range(SLOTS):
                gather(Group(0, g), range(TG))
            for k in range(1, KP, 2):
                pool.wait_ge(z_hi_ready, k + 1)
                nc.gpsimd.tensor_tensor(z_lo[:, k, :], z[:, k, :], z_hi[:, k, :].bitcast(F32),
                                        ALU.subtract).then_inc(first_odd_z_lo, 1)
            pool.wait_ge(z_lo_ready, KP - KP // 2)
            pool.wait_ge(first_odd_z_lo, KP // 2)
            pool.sem_inc(z_lo_ready, KP // 2)

            def body(g, number):
                for u in range(TG):
                    if not (number == 0 and u == 0):
                        add(*before(g, u))
                    if u < 2 and (number is None or number + 1 < GROUPS):
                        split_z(g.plus(1), 2 * u)
                        split_z(g.plus(1), 2 * u + 1)
                    if u == 2 and (number is None or number + 1 < GROUPS):
                        split_z(g.plus(1), LASTK)
                    if u >= 2 and (number is None or number + SLOTS < GROUPS):
                        gather(g.plus(SLOTS), ((0, 1), (2, 3))[u - 2])
                    if number == GROUPS - 1 and u >= 2:
                        low, whole, high = ((wt2_lo, wt2_sb[:, :, :], wt2_hi), (wt1_lo, wt1_sb[:, 1, :], wt1_hi))[u - 2]
                        pool.wait_ge(top_hi_ready, u - 1)
                        nc.gpsimd.tensor_tensor(low, whole, high.bitcast(F32), ALU.subtract).then_inc(top_lo_ready, 1)

            over_groups(pool, body)
            add(LAST, TG - 1, *ADDS_LAST[0])
            pool.wait_ge(added, TILES)
            add(LAST, TG - 1, *ADDS_LAST[1])

        @block.scalar
        def _(act):
            def split_z(g, k):
                act.wait_ge(z_ready, g.times(KP, k + 1))
                wait(act, l0_done, g.times(1))
                nc.scalar.activation(z_hi[:, k, :], z[:, k, :], ACT.Copy,
                                     scale=copy_sb[:, 0:1] if k == LASTK else 1.0).then_inc(z_hi_ready, 1)

            def rectify(g, tiles=slice(0, TG), hi_ready=c_hi_ready, ready=c_ready):
                act.wait_ge(l0_done, g.times(1, 1))
                out = ps_c[:, :].rearrange("p (b u d) -> p b u d", u=TG, b=BT)[:, :, tiles, :]
                nc.scalar.activation(c_hi[:, g.r, :].rearrange("p (u b d) -> p b u d", u=TG, b=BT)[:, :, tiles, :],
                                     out, ACT.Relu).then_inc(hi_ready, 1)
                wait(act, h0_done, g.times(1))
                nc.scalar.activation(c[:, :].rearrange("p (b u d) -> p b u d", u=TG, b=BT)[:, :, tiles, :],
                                     out, ACT.Relu).then_inc(ready, 1)

            def scale(g, u, k):
                if k == ACT_BANKS[u][0]:
                    if u == 0:
                        act.wait_ge(es_ready, g.times(1, 1))
                    wait(act, reduced, g.times(TG * HALVES, (u + 1 - BUFS) * HALVES))
                act.wait_ge(y_ready, g.times(TG * NK, u * NK + k + 1))
                for j in range(HB):
                    h = HB * k + j
                    last = nc.scalar.activation(prod[:, buffer_of(g, u), h, :],
                                                ps_y[:, bank_of(g, u, k), j * N:(j + 1) * N], ACT.Copy,
                                                scale=es[:, g.r, u, h:h + 1])
                last.then_inc(act_scaled, 1)

            for k in range(NK):
                act.wait_ge(w1_in[k * W1_LOADS // NK], 16)
                nc.scalar.activation(w1_hi[:, k * HB:(k + 1) * HB, :], w1_raw[:, k * HB:(k + 1) * HB, :],
                                     ACT.Copy).then_inc(w1_hi_ready, 1)
            for k in range(KP):
                if k == LASTK:
                    act.wait_ge(w0_in, 48)
                split_z(Group(0, 0), k)
            rectify(Group(0, 0), slice(0, 1), first_c_hi, first_c)
            rectify(Group(0, 0), slice(1, TG))
            act.wait_ge(w_ready, 3)

            def body(g, number):
                more = number is None or number + 1 < GROUPS
                for u in range(TG):
                    for k in range(NK):
                        if k in ACT_BANKS[u]:
                            scale(g, u, k)
                        for (n, chunk), at in (Z_HI_AT_FIRST if number == 0 else Z_HI_AT).items():
                            if at == (u, k) and (number is None or number + n < GROUPS):
                                split_z(g.plus(n), chunk)
                        if more and (u, k) == (3, 1):
                            rectify(g.plus(1))

            Z_HI_AT_FIRST = {(1, 0): (0, 3), (1, 1): (0, 5), (1, 2): (0, 7), (1, 3): (1, 1), (1, 4): (1, 5), (2, 0): (3, 4), (2, 1): (3, 7)}
            Z_HI_AT = {(2, 0): (3, 4), (2, 1): (3, 7), (1, 2): (0, 2), (1, 3): (0, 5), (1, 4): (1, 5)}
            over_groups(act, body)

            for tiles in (range(TILES - 2), range(TILES - 2, TILES)):
                act.wait_ge(h1_done, tiles.stop)
                cols = slice(BT * tiles.start, BT * tiles.stop)
                nc.scalar.activation(h1_hi[:, cols], ps_h1[:, cols], ACT.Copy).then_inc(h1_hi_ready, 1)
            act.wait_ge(top_in, 7 * 16)
            for j in range(TOP1 // P):
                act.wait_ge(mm_top, j + 1)
                nc.scalar.activation(a1_hi[:, j, :], ps_a1[j], ACT.Relu, bias=bt1_sb[:, j:j + 1]).then_inc(a1_hi_ready, 1)
                nc.scalar.activation(a1[:, j, :], ps_a1[j], ACT.Relu, bias=bt1_sb[:, j:j + 1]).then_inc(a1_ready, 1)
            for j in range(TOP2 // P):
                act.wait_ge(mm_top, 5 + j)
                nc.scalar.activation(a2[:, j, :], ps_a2[j], ACT.Relu, bias=bt2_sb[:, j:j + 1]).then_inc(act_top, 1)
            act.wait_ge(mm_top, 7)
            nc.scalar.activation(y_sb[:, :], ps_c[0:1, :], ACT.Copy).then_inc(act_top, 1)

        @block.vector
        def _(dve):
            dve.wait_ge(ids_in, 32)
            nc.vector.tensor_copy(idf[:, :], ids_sb[:, :]).then_inc(rows_step, 1)
            dve.wait_ge(rows_step, 1)
            nc.vector.tensor_scalar(neg[:, :], idf[:, :], 0.0, bounds_sb[:, 1:2], ALU.is_lt, ALU.mult).then_inc(rows_step, 1)
            dve.wait_ge(rows_step, 2)
            nc.vector.tensor_tensor(idf[:, :], idf[:, :], neg[:, :], ALU.add).then_inc(rows_step, 1)
            dve.wait_ge(rows_step, 3)
            nc.vector.tensor_scalar(neg[:, :], idf[:, :], 0.0, bounds_sb[:, 0:1], ALU.max, ALU.min).then_inc(rows_step, 1)
            dve.wait_ge(rows_step, 4)
            nc.vector.tensor_scalar(rows[:, :], neg[:, :], bounds_sb[:, 2:3], None, ALU.add).then_inc(rows_step, 1)

            nc.vector.memset(ones_b[:, :], 0.0).then_inc(ones_zeroed, 1)
            dve.wait_ge(ones_zeroed, 1)
            for b in range(BT):
                nc.vector.memset(ones_b[b * D:(b + 1) * D, b:b + 1], 1.0).then_inc(ones_zeroed, 1)

            dve.wait_ge(w0_in, 48)
            nc.vector.tensor_tensor(w0_sum[:, :, :], w0a_sb, w0b_sb, ALU.add).then_inc(w0_step, 1)
            dve.wait_ge(w0_step, 1)
            nc.vector.tensor_copy(w0_hi[:, :, :], w0_sum[:, :, :]).then_inc(w0_step, 1)
            dve.wait_ge(w0_step, 2)
            nc.vector.tensor_tensor(w0_lo[:, 0:LASTK, :], w0_sum[:, 0:LASTK, :], w0_hi[:, 0:LASTK, :].bitcast(F32),
                                    ALU.subtract).then_inc(w_ready, 1)
            nc.vector.scalar_tensor_tensor(out=w0_lo[:, LASTK, :], in0=w0_hi[:, LASTK, :].bitcast(F32), scalar=copy_sb[:, 1:2],
                                           in1=w0_sum[:, LASTK, :], op0=ALU.mult, op1=ALU.add).then_inc(w_ready, 1)

            def turn(g):
                dve.wait_ge(gathered[g.r], g.uses(16 * TG))
                nc.vector.transpose(es[:, g.r, :, :].rearrange("p u f -> p (u f)"), gat[:, g.r, :]).then_inc(es_ready, 1)

            def multiply(g, k):
                dve.wait_ge(pairs_in[k], g.times(32, 32) if k == 0 else g.times(16, 16))
                wait(dve, z_lo_ready, g.times(KP, k + 1 - KP))
                nc.vector.tensor_tensor(z[:, k, :], first[:, :], second[:, k, :], ALU.mult).then_inc(z_ready, 1)

            def split_c(g, tiles=slice(0, TG), ready=c_ready, lo_ready=c_lo_ready):
                dve.wait_ge(ready, g.times(1, 1))
                nc.vector.tensor_tensor(
                    c_lo[:, g.r, :].rearrange("p (u b d) -> p b u d", u=TG, b=BT)[:, :, tiles, :],
                    c[:, :].rearrange("p (b u d) -> p b u d", u=TG, b=BT)[:, :, tiles, :],
                    c_hi[:, g.r, :].bitcast(F32).rearrange("p (u b d) -> p b u d", u=TG, b=BT)[:, :, tiles, :],
                    ALU.subtract).then_inc(lo_ready, 1)

            def sum_h0(g):
                nc.vector.tensor_reduce(
                    h0[:, bass.ds(g.times(TG * BT), TG * BT)].rearrange("p (u b) -> p b u", u=TG),
                    c[:, :].rearrange("p (b u d) -> p b u d", u=TG, b=BT), AX.X, ALU.add).then_inc(h0_done, 1)

            def scale(g, u, k):
                if k == DVE_BANKS[u][0]:
                    if u == 0:
                        dve.wait_ge(es_ready, g.times(1, 1))
                    wait(dve, reduced, g.times(TG * HALVES, (u + 1 - BUFS) * HALVES))
                dve.wait_ge(y_ready, g.times(TG * NK, u * NK + k + 1))
                fields = slice(HB * k, HB * (k + 1))
                nc.vector.tensor_tensor(
                    prod[:, buffer_of(g, u), fields, :],
                    ps_y[:, bank_of(g, u, k), :].rearrange("p (h n) -> p h n", n=N),
                    es[:, g.r, u, fields].unsqueeze(2).to_broadcast([P, HB, N]), ALU.mult).then_inc(dve_scaled, 1)

            def reduce(g, u, half, start=ADD, additions=1):
                if half == 0:
                    dve.wait_ge(added, g.times(TG, u + additions))
                    dve.wait_ge(act_scaled, signals(ACT_BANKS, g, u, NK - 1))
                    dve.wait_ge(dve_scaled, signals(DVE_BANKS, g, u, NK - 1))
                    wait(dve, c1_ready, g.times(TG, u))
                maps = slice(half * N // HALVES, (half + 1) * N // HALVES)
                nc.vector.tensor_reduce(csum[:, maps], prod[:, buffer_of(g, u), start:F, maps].rearrange("p h n -> p n h"),
                                        AX.X, ALU.add).then_inc(reduced, 1)

            def rectify(g, u):
                dve.wait_ge(reduced, g.times(TG * HALVES, (u + 1) * HALVES))
                wait(dve, h1_done, g.times(TG, u - 1))
                nc.vector.tensor_scalar(c1[:, u % 2, :], csum[:, :], 0.0, None, ALU.max).then_inc(c1_ready, 1)

            for k in range(NK):
                dve.wait_ge(w1_hi_ready, k + 1)
                part = slice(k * HB, (k + 1) * HB)
                last = nc.vector.tensor_tensor(w1_lo[:, part, :], w1_raw[:, part, :],
                                               w1_hi[:, part, :].bitcast(F32), ALU.subtract)
            last.then_inc(w_ready, 1)
            turn(Group(0, 0))
            multiply(Group(0, 0), 0)
            multiply(Group(0, 0), 1)
            for k in range(0, KP, 2):
                dve.wait_ge(z_hi_ready, k + 1)
                nc.vector.tensor_tensor(z_lo[:, k, :], z[:, k, :], z_hi[:, k, :].bitcast(F32),
                                        ALU.subtract).then_inc(z_lo_ready, 1)
                for chunk in range(k + 2, min(k + 4, KP)):
                    multiply(Group(0, 0), chunk)
            split_c(Group(0, 0), slice(0, 1), first_c, first_c_lo)
            split_c(Group(0, 0), slice(1, TG))
            sum_h0(Group(0, 0))
            dve.wait_ge(z_lo_ready, KP)
            dve.wait_ge(w_ready, 3)

            def round_top(out, whole):
                dve.wait_ge(top_in, 7 * 16)
                dve.wait_ge(l0_done, GROUPS)
                nc.vector.tensor_copy(out, whole).then_inc(top_hi_ready, 1)

            Z_AT_FIRST = {(1, 0): (0, 2), (1, 1): (0, 4), (1, 2): (0, 6), (1, 3): (0, 7), (1, 4): (1, 3), (2, 0): (3, 0), (2, 1): (3, 3)}
            Z_AT = {(2, 0): (3, 0), (2, 1): (3, 3), (1, 2): (0, 0), (1, 3): (0, 3), (1, 4): (1, 3)}

            def body(g, number):
                more = number is None or number + 1 < GROUPS
                for u in range(TG):
                    for k in range(NK):
                        if k in DVE_BANKS[u]:
                            scale(g, u, k)
                        if k == 2 and not (number == 0 and u < 2):
                            reduce(*before(g, u, 2), 1)
                        if k == 4 and not (number == 0 and u < 2):
                            rectify(*before(g, u, 2))
                        if k == 6 and not (number == 0 and u == 0):
                            reduce(*before(g, u), 0)
                        for (n, chunk), at in (Z_AT_FIRST if number == 0 else Z_AT).items():
                            if at == (u, k) and (number is None or number + n < GROUPS):
                                multiply(g.plus(n), chunk)
                        if number == GROUPS - 1 and (u, k) == (1, 3):
                            round_top(wt2_hi, wt2_sb[:, :, :])
                        if number == GROUPS - 1 and (u, k) == (2, 3):
                            round_top(wt1_hi, wt1_sb[:, 1, :])
                        if more and (u, k) == (2, 3):
                            turn(g.plus(1))
                        if more and (u, k) == (3, 3):
                            split_c(g.plus(1))
                        if more and (u, k) == (3, 5):
                            sum_h0(g.plus(1))

            over_groups(dve, body)
            reduce(LAST, TG - 2, 1)
            rectify(LAST, TG - 2)
            for half in range(HALVES):
                reduce(LAST, TG - 1, half, ADDS_LAST[-1][1], len(ADDS_LAST))
            rectify(LAST, TG - 1)
            dve.wait_ge(h1_hi_ready, 2)
            nc.vector.tensor_tensor(h1_lo, ps_h1[:, :], h1_hi.bitcast(F32), ALU.subtract).then_inc(h1_lo_ready, 1)
            for j in range(TOP1 // P):
                dve.wait_ge(a1_ready, j + 1)
                nc.vector.tensor_tensor(a1_lo[:, j, :], a1[:, j, :], a1_hi[:, j, :].bitcast(F32),
                                        ALU.subtract).then_inc(a1_lo_ready, 1)

        @block.tensor
        def _(pe):
            def layer0(g, k, number=None):
                if k == 0:
                    wait(pe, c_ready, g.times(1))
                if number == 0 and k % 2:
                    pe.wait_ge(first_odd_z_lo, k // 2 + 1)
                elif number == 0:
                    pe.wait_ge(z_lo_ready, k // 2 + 1)
                else:
                    pe.wait_ge(z_lo_ready, g.times(KP, k + 1))
                if k == LASTK:
                    nc.tensor.matmul(ps_c[:, :], w0_lo[:, k, :], z_lo[:, k, :], start=False, stop=True).then_inc(l0_done, 1)
                    return
                nc.tensor.matmul(ps_c[:, :], w0_hi[:, k, :], z_hi[:, k, :], start=(k == 0), stop=False)
                nc.tensor.matmul(ps_c[:, :], w0_lo[:, k, :], z_hi[:, k, :], start=False, stop=False)
                nc.tensor.matmul(ps_c[:, :], w0_hi[:, k, :], z_lo[:, k, :], start=False, stop=False)

            def layer1(g, u, k, number):
                if number is None or number > 0 or NK * u + k >= RING:
                    wait(pe, act_scaled, signals(ACT_BANKS, g, u, k - RING))
                    wait(pe, dve_scaled, signals(DVE_BANKS, g, u, k - RING))
                out = ps_y[:, bank_of(g, u, k), :]
                hi, lo = (x[:, g.r, u * P:(u + 1) * P] for x in (c_hi, c_lo))
                w_hi, w_lo = (x[:, k * HB:(k + 1) * HB, :].rearrange("p h n -> p (h n)") for x in (w1_hi, w1_lo))
                nc.tensor.matmul(out, hi, w_hi, start=True, stop=False)
                nc.tensor.matmul(out, hi, w_lo, start=False, stop=False)
                if number == 0 and u == 0 and k == 0:
                    pe.wait_ge(first_c_lo, 1)
                elif k == 0 and u == (1 if number == 0 else 0):
                    pe.wait_ge(c_lo_ready, g.times(1, 1))
                nc.tensor.matmul(out, lo, w_hi, start=False, stop=True).then_inc(y_ready, 1)

            def sum_h1(g, u):
                pe.wait_ge(c1_ready, g.times(TG, u + 1))
                nc.tensor.matmul(ps_h1[:, bass.ds(g.times(TG * BT, u * BT), BT)], c1[:, u % 2, :], ones_b[:, :],
                                 start=True, stop=True).then_inc(h1_done, 1)

            pe.wait_ge(ones_zeroed, 1 + BT)
            pe.wait_ge(w_ready, 2)
            pe.wait_ge(es_ready, 1)
            for n in range(WARM_UP):
                nc.tensor.matmul(ps_y[:, 0, :], w0_hi[:, 0, :], w0_hi[:, 0:BANK // N, :].rearrange("p k n -> p (k n)"),
                                 start=True, stop=True)
            for k in range(KP):
                layer0(Group(0, 0), k, 0)
            pe.wait_ge(w_ready, 3)

            Z_USED_AT_FIRST = ((1, 4), (1, 7), (2, 2), (2, 5), (2, 7))
            Z_USED_AT = ((1, 1), (1, 4), (2, 1), (2, 4), (2, 6))

            def body(g, number):
                more = number is None or number + 1 < GROUPS
                z_used_at = Z_USED_AT_FIRST if number == 0 else Z_USED_AT
                for u in range(TG):
                    if number == 0 and u == 0:
                        pe.wait_ge(first_c_hi, 1)
                    elif u == (1 if number == 0 else 0):
                        pe.wait_ge(c_hi_ready, g.times(1, 1))
                    for k in range(NK):
                        layer1(g, u, k, number)
                        if more and (u, k) in z_used_at:
                            layer0(g.plus(1), z_used_at.index((u, k)))
                        if k == 3 and not (number == 0 and u < 3):
                            sum_h1(*before(g, u, 3))

            over_groups(pe, body)
            sum_h1(LAST, TG - 3)

            pe.wait_ge(top_in, 7 * 16)
            pe.wait_ge(h0_done, GROUPS)
            for j in range(TOP1 // P):
                pe.wait_ge(act_scaled, signals(ACT_BANKS, LAST, TG - 1, NK - RING + j))
                pe.wait_ge(dve_scaled, signals(DVE_BANKS, LAST, TG - 1, NK - RING + j))
                cols = slice(j * P, (j + 1) * P)
                nc.tensor.matmul(ps_a1[j], wt1_sb[:, 0, cols], h0[:, :], start=True, stop=False)
                nc.tensor.matmul(ps_a1[j], wt1_d[:, cols], hd[:, :], start=False, stop=False)
            pe.wait_ge(h1_hi_ready, 1)
            sum_h1(LAST, TG - 2)
            sum_h1(LAST, TG - 1)
            pe.wait_ge(top_lo_ready, 2)
            pe.wait_ge(h1_hi_ready, 2)
            for j in range(TOP1 // P):
                nc.tensor.matmul(ps_a1[j], wt1_hi[:, j * P:(j + 1) * P], h1_hi, start=False, stop=False)
                nc.tensor.matmul(ps_a1[j], wt1_lo[:, j * P:(j + 1) * P], h1_hi, start=False, stop=False)
            pe.wait_ge(h1_lo_ready, 1)
            for j in range(TOP1 // P):
                nc.tensor.matmul(ps_a1[j], wt1_hi[:, j * P:(j + 1) * P], h1_lo, start=False, stop=True).then_inc(mm_top, 1)
            for k in range(TOP1 // P):
                pe.wait_ge(a1_hi_ready, k + 1)
                for j in range(TOP2 // P):
                    cols = slice(j * P, (j + 1) * P)
                    nc.tensor.matmul(ps_a2[j], wt2_hi[:, k, cols], a1_hi[:, k, :], start=(k == 0), stop=False)
                    nc.tensor.matmul(ps_a2[j], wt2_lo[:, k, cols], a1_hi[:, k, :], start=False, stop=False)
                pe.wait_ge(a1_lo_ready, k + 1)
                for j in range(TOP2 // P):
                    last = nc.tensor.matmul(ps_a2[j], wt2_hi[:, k, j * P:(j + 1) * P], a1_lo[:, k, :],
                                            start=False, stop=(k == TOP1 // P - 1))
                    if k == TOP1 // P - 1:
                        last.then_inc(mm_top, 1)
            for k in range(TOP2 // P):
                pe.wait_ge(act_top, k + 1)
                last = nc.tensor.matmul(ps_c[0:1, :], wt3_sb[:, k:k + 1], a2[:, k, :],
                                        start=(k == 0), stop=(k == TOP2 // P - 1))
            last.then_inc(mm_top, 1)


def pair_rows():
    a = np.full((F, SH, KP), F * F)
    b = np.full((F, SH, KP), F * F)
    for k in range(KP):
        for s in range(SH):
            dist = SH * k + (s if k < LASTK else 0)
            if k == LASTK and s == SH - 1:
                continue
            for h in range(F):
                m = (h + dist) % F
                if dist < F // 2 or (dist == F // 2 and h < F // 2):
                    a[h, s, k] = F * h + m
                    if dist:
                        b[h, s, k] = F * m + h
    return a.reshape(P, KP), b.reshape(P, KP)


def kernel(**inputs):
    import concourse.bacc as bacc
    from concourse.bass_utils import run_bass_kernel_spmd

    x = {name: np.asarray(a) for name, a in inputs.items()}
    tables = [x[f"tbl_{f}"] for f in range(F)]
    counts = np.array([t.shape[0] for t in tables])
    bases = np.cumsum(counts) - counts
    rows_a, rows_b = pair_rows()
    w0 = np.concatenate([x["L0_rec_filter_0"][0], np.zeros((1, N), np.float32)])
    arrays = {
        "ids": np.ascontiguousarray(x["ids"].reshape(TILES, BT, F).transpose(1, 2, 0).reshape(P, TILES)),
        "bounds": np.tile(np.stack([counts - 1, counts, bases], 1).astype(np.float32), (BT, 1)),
        "copy_of": np.tile(np.array([[0, 0], [1, 0], [0, -1], [0, 0]], np.float32), (F, 1)),
        "table": np.concatenate(tables),
        "dense_t": np.ascontiguousarray(x["dense_ctx"].T),
        "w0a": w0[rows_a],
        "w0b": w0[rows_b],
        "w1": np.ascontiguousarray(x["L0_rec_filter_1"][0]),
        "wt1": x["W_top1"],
        "bt1": np.ascontiguousarray(x["b_top1"].reshape(TOP1 // P, P).T),
        "wt2": x["W_top2"],
        "bt2": np.ascontiguousarray(x["b_top2"].reshape(TOP2 // P, P).T),
        "wt3": np.ascontiguousarray(x["W_top3"].reshape(TOP2 // P, P).T),
    }
    nc = bacc.Bacc("TRN2", target_bir_lowering=False, num_devices=1)
    args = [nc.dram_tensor(n, a.shape, mybir.dt.from_np(a.dtype), kind="ExternalInput").ap() for n, a in arrays.items()]
    y = nc.dram_tensor("y", (1, B), F32, kind="ExternalOutput").ap()
    tower(nc, *args, y)
    r = run_bass_kernel_spmd(nc, [arrays], core_ids=[0])
    return r.results[0]["y"].reshape(B, 1)
```
